# Optimizing a Trainium2 kernel written in Bass

```python
import numpy as np
import jax
import jax.numpy as jnp

def _softmax(x, axis=-1):
    return jax.nn.softmax(x, axis=axis)

def _gelu(x):
    return jax.nn.gelu(x, approximate=True)

def _silu(x):
    return jax.nn.silu(x)

def _sigmoid(x):
    return jax.nn.sigmoid(x)

def _layernorm(x, axis=-1, eps=1e-05):
    m = jnp.mean(x, axis=axis, keepdims=True)
    v = jnp.var(x, axis=axis, keepdims=True)
    return (x - m) / jnp.sqrt(v + eps)

def _scatter_add(tgt, idx, src, axis=0):
    return tgt.at[idx].add(src)

def _segment_sum(src, seg, n):
    return jax.ops.segment_sum(src, seg, n)
kernel_name = 'mk_macaron_d1_jaxref_r8_c5fa5e'

def setup_inputs(seed: int=0):
    np.random.seed(seed)
    _w = jnp.asarray

    def _L0_attn_setup():
        import jax, jax.numpy as jnp
        import numpy as np
        import math
        T = 0.28
        EPS = 1e-06
        D_MODEL = 128
        N_HEADS = 16
        D_K = D_MODEL // N_HEADS

        def compute_radius(t, epsilon):
            raw = math.sqrt(4.0 * t * math.log(1.0 / epsilon))
            return max(int(math.ceil(raw * 2.0)), 1)
        RADIUS = compute_radius(T, EPS)
        WIN = RADIUS + 1
        key = jax.random.key(seed)
        ks = jax.random.split(key, 5)
        B, S = (2, 512)
        x = jax.random.normal(ks[0], (B, S, D_MODEL), dtype=jnp.float32)
        scale = 1.0 / math.sqrt(D_MODEL)
        Wq = jax.random.normal(ks[1], (D_MODEL, D_MODEL), dtype=jnp.float32) * scale
        Wk = jax.random.normal(ks[2], (D_MODEL, D_MODEL), dtype=jnp.float32) * scale
        Wv = jax.random.normal(ks[3], (D_MODEL, D_MODEL), dtype=jnp.float32) * scale
        Wo = jax.random.normal(ks[4], (D_MODEL, D_MODEL), dtype=jnp.float32) * scale
        return {'x': x, 'Wq': Wq, 'Wk': Wk, 'Wv': Wv, 'Wo': Wo}
    _L0_attn_in = _L0_attn_setup()

    def _L0_ffn_setup():
        import jax, jax.numpy as jnp
        import numpy as np
        D = 128
        H = 512
        E = 8
        K = 2
        B, S = (4, 256)
        key = jax.random.key(seed)
        ks = jax.random.split(key, 8)

        def lin(k, fan_in, shape):
            bound = 1.0 / np.sqrt(fan_in)
            return jax.random.uniform(k, shape, jnp.float32, -bound, bound)
        return {'x': jax.random.normal(ks[0], (B, S, D), jnp.float32), 'Wg': lin(ks[1], D, (D, E)), 'bg': lin(ks[2], D, (E,)), 'W1': lin(ks[3], D, (E, D, H)), 'b1': lin(ks[4], D, (E, H)), 'W2': lin(ks[5], H, (E, H, D)), 'b2': lin(ks[6], H, (E, D))}
    _L0_ffn_in = _L0_ffn_setup()
    _d = {'L0_attn_x': _L0_attn_in['x'], 'L0_attn_Wq': _L0_attn_in['Wq'], 'L0_attn_Wk': _L0_attn_in['Wk'], 'L0_attn_Wv': _L0_attn_in['Wv'], 'L0_attn_Wo': _L0_attn_in['Wo'], 'L0_ffn_Wg': _L0_ffn_in['Wg'], 'L0_ffn_bg': _L0_ffn_in['bg'], 'L0_ffn_W1': _L0_ffn_in['W1'], 'L0_ffn_b1': _L0_ffn_in['b1'], 'L0_ffn_W2': _L0_ffn_in['W2'], 'L0_ffn_b2': _L0_ffn_in['b2']}
    _x0 = _d['L0_attn_x']
    _d['L0_attn_x'] = jax.random.normal(jax.random.fold_in(jax.random.key(seed), 1), (32, 256, 128), dtype=_x0.dtype)
    del _x0
    return _d

def reference(L0_attn_x, L0_attn_Wq, L0_attn_Wk, L0_attn_Wv, L0_attn_Wo, L0_ffn_Wg, L0_ffn_bg, L0_ffn_W1, L0_ffn_b1, L0_ffn_W2, L0_ffn_b2):

    def _L0_attn_ref(x, Wq, Wk, Wv, Wo):
        import jax, jax.numpy as jnp
        import numpy as np
        import math
        T = 0.28
        EPS = 1e-06
        D_MODEL = 128
        N_HEADS = 16
        D_K = D_MODEL // N_HEADS

        def compute_radius(t, epsilon):
            raw = math.sqrt(4.0 * t * math.log(1.0 / epsilon))
            return max(int(math.ceil(raw * 2.0)), 1)
        RADIUS = compute_radius(T, EPS)
        WIN = RADIUS + 1
        B, S, _ = x.shape

        def split_heads(h):
            return h.reshape(B, S, N_HEADS, D_K).transpose(0, 2, 1, 3)
        q = split_heads(x @ Wq)
        k = split_heads(x @ Wk)
        v = split_heads(x @ Wv)
        pos = jnp.arange(S)
        idx = pos[:, None] + jnp.arange(-RADIUS, 1)[None, :]
        valid = idx >= 0
        idx_c = jnp.clip(idx, 0, S - 1)
        k_win = k[:, :, idx_c, :]
        v_win = v[:, :, idx_c, :]
        scores = jnp.einsum('bhsd,bhswd->bhsw', q, k_win) / (2.0 * T)
        scores = jnp.where(valid[None, None, :, :], scores, -jnp.inf)
        wts = jax.nn.softmax(scores, axis=-1)
        wts = jnp.nan_to_num(wts, nan=0.0)
        attn = jnp.einsum('bhsw,bhswd->bhsd', wts, v_win)
        attn = attn.transpose(0, 2, 1, 3).reshape(B, S, D_MODEL)
        return attn @ Wo

    def _L0_ffn_ref(x, Wg, bg, W1, b1, W2, b2):
        import jax, jax.numpy as jnp
        import numpy as np
        D = 128
        H = 512
        E = 8
        K = 2
        B, S = (4, 256)
        B_, S_, D_ = x.shape
        xt = x.reshape(-1, D_)
        logits = xt @ Wg + bg
        scores = jax.nn.softmax(logits, axis=-1)
        topk_probs, topk_idx = jax.lax.top_k(scores, K)
        h = jnp.einsum('nd,edh->enh', xt, W1) + b1[:, None, :]
        h = jax.nn.gelu(h, approximate=False)
        eo = jnp.einsum('enh,ehd->end', h, W2) + b2[:, None, :]
        eo = jnp.transpose(eo, (1, 0, 2))
        sel = jnp.take_along_axis(eo, topk_idx[:, :, None], axis=1)
        out = jnp.einsum('nk,nkd->nd', topk_probs, sel)
        return out.reshape(B_, S_, D_)
    x = L0_attn_x
    x = x + 0.5 * _L0_ffn_ref(_layernorm(x, axis=-1), L0_ffn_Wg, L0_ffn_bg, L0_ffn_W1, L0_ffn_b1, L0_ffn_W2, L0_ffn_b2)
    x = x + _L0_attn_ref(_layernorm(x, axis=-1), L0_attn_Wq, L0_attn_Wk, L0_attn_Wv, L0_attn_Wo)
    x = x + 0.5 * _L0_ffn_ref(_layernorm(x, axis=-1), L0_ffn_Wg, L0_ffn_bg, L0_ffn_W1, L0_ffn_b1, L0_ffn_W2, L0_ffn_b2)
    return x

_drawn_inputs = setup_inputs


def setup_inputs(seed=0):
    import zlib

    import numpy as np

    out = dict(_drawn_inputs(seed))
    spreads = {}
    factors = {'L0_ffn_bg': 4.247, 'L0_ffn_b1': 8.0, 'L0_ffn_b2': 6.171}
    for name, (base, spread) in spreads.items():
        noise = np.random.default_rng([zlib.crc32(name.encode()), seed]).standard_normal(out[name].shape)
        drawn = base * np.exp(spread * noise) if base else spread * noise
        out[name] = jnp.asarray(drawn.astype(out[name].dtype))
    for name, factor in factors.items():
        out[name] = (out[name] * factor).astype(out[name].dtype)
    return out
```

```python
from contextlib import ExitStack

import concourse.bass as bass
from concourse import mybir

F32 = mybir.dt.float32
F16 = mybir.dt.float16
BF16 = mybir.dt.bfloat16
I32 = mybir.dt.int32
U32 = mybir.dt.uint32
ALU = mybir.AluOpType
ACT = mybir.ActivationFunctionType
X = mybir.AxisListType.X

P = 128
D = 128
E = 8
H = 512
HC = H // P
HEADS = 16
DK = D // HEADS
RADIUS = 8
W = RADIUS + 1
SCORE_SCALE = 1.0 / (2.0 * 0.28)
LN_EPS = 1e-5
WS = 64.0
LOW = -1e30
J = 16
C = 4
JC = J // C
SLOT_TILE = 256
NJ = 4
SPARE = 12
EU = 8
PEEL = 6
Y_LAG = 6
TOK_RING = 8
ROUTE_STEPS = 56
GROUP_STEPS = 117
PLAN_STEPS = 33
DMA = 16


class Steps:

    def __init__(self, eng, sem, before):
        self.eng, self.sem, self.before, self.n = eng, sem, before, 0

    def did(self, ins):
        ins.then_inc(self.sem, 1)
        self.n += 1

    def settle(self):
        self.eng.wait_ge(self.sem, self.before + self.n)


class Tile:

    def __init__(self, i, first, f, n_tiles):
        def uses(n):
            return i * (EU // n) + (first // n + f * len(range(first % n, n_tiles, n)))
        self.j = i * EU + first
        self.ring, self.ring_uses = first % 4, uses(4)
        self.par, self.par_uses = first % 2, uses(2)
        self.tok, self.tok_uses = first % TOK_RING, uses(TOK_RING)
        self.first_of_body = not isinstance(i, int) and first == PEEL or isinstance(i, int) and first > PEEL and (first - PEEL) % EU == 0
        self.count = i * EU + (first + f * n_tiles)
        self.not_first = f > 0 or first > 0
        self.ring_reused = f > 0 or first >= 4
        self.par_reused = f > 0 or first >= 2


def macaron(nc, x, Wq, Wk, Wv, Wo, Wg, bg, W1, b1, W2, b2, out):
    B, S, _ = x.shape
    N = B * S
    G = N // (P * J)
    TILES = G * J
    NT = (2 * N - E) // SLOT_TILE + E
    LOOPS = (NT - PEEL - 1) // EU
    SLOTS = E * N + SPARE * SLOT_TILE
    SP_COLS = SLOTS // P
    LOW_SEQ = S // J

    x_hl = nc.dram_tensor("x_hl", [N, 2 * D], F16, kind="Internal").ap()
    slot_token = [nc.dram_tensor(f"slot_token{r}", [SLOTS], U32, kind="Internal").ap() for r in range(NJ)]
    slot_token_sum = nc.dram_tensor("slot_token_sum", [SLOTS], U32, kind="Internal").ap()
    y_rows = nc.dram_tensor("y_rows", [NT * SLOT_TILE, D], F32, kind="Internal").ap()

    x_v = x.flatten_outer_dims().rearrange("(g p j) d -> g p (j d)", p=P, j=J)
    out_v = out.flatten_outer_dims().rearrange("(g p j) d -> g p (j d)", p=P, j=J)
    x_hl_v = x_hl.rearrange("(g p j) c -> g p (j c)", p=P, j=J)

    with ExitStack() as ctx:
        def sb(name, shape, dt):
            return ctx.enter_context(nc.sbuf_tensor(name, shape, dt))

        def sem(name):
            return ctx.enter_context(nc.semaphore(name))

        def sems(name, n):
            return [sem(f"{name}{i}") for i in range(n)]

        x_sb = sb("x_sb", [P, TILES * D], F32)
        w1_hl = sb("w1_hl", [P, 2, E * H], F16)
        w2_hl = sb("w2_hl", [P, 2, E * HC * D], F16)
        wqkv = sb("wqkv", [P, 3 * D], F32)
        wo_sb = sb("wo_sb", [P, D], F32)
        wg_sb = sb("wg_sb", [P, E], F32)
        bg_bc = sb("bg_bc", [P, E], F32)
        b1_rows = sb("b1_rows", [E * HC, P], F32)
        b1_cols = sb("b1_cols", [P, E * HC], F32)
        b2_bc = sb("b2_bc", [P, E * D], F32)
        ident = sb("ident", [P, P], F32)
        ident16 = sb("ident16", [P, P], F16)
        before16 = sb("before16", [P, P], BF16)
        ones16 = sb("ones16", [P, P], BF16)
        e_iota = sb("e_iota", [P, J * E], F32)
        token_ids = sb("token_ids", [P, TILES], U32)
        window_mask = sb("window_mask", [P, RADIUS * W], F32)
        part_i = sb("part_i", [P, 1], I32)
        seq_start = sb("seq_start", [P, 1], F32)
        gates = sb("gates", [P, TILES * 2], F32)
        slots_all = sb("slots_all", [P, TILES * 2], F32)
        y_row = sb("y_row", [P, (TILES + J) * 2], U32)
        stats = sb("stats", [P, J, 6], F32)
        mean_var = sb("mean_var", [P, J, 2], F32)
        var_eps = sb("var_eps", [P, J], F32)
        std = sb("std", [P, J], F32)
        rstd = sb("rstd", [P, J], F32)
        xn = sb("xn", [P, J, D], F32)
        xnT = sb("xnT", [P, J, D + 2], F32)
        hl = sb("hl", [P, J, 2 * D], F16)
        logits = sb("logits", [P, J * E], F32)
        top = sb("top", [P, 2, J], F32)
        cand = sb("cand", [P, J * E], F32)
        cand2 = sb("cand2", [P, J * E], F32)
        choice = sb("choice", [P, 2, J], F32)
        onehot = sb("onehot", [P, J, 2, E], F32)
        logits2 = sb("logits2", [P, J * E], F32)
        gate_exp = sb("gate_exp", [P, J, E + 1], F32)
        gate_sum = sb("gate_sum", [P, J], F32)
        gate_inv = sb("gate_inv", [P, J], F32)
        chosen = sb("chosen", [P, (J + 1) * E], BF16)
        slot_base = sb("slot_base", [P, 2, E], F32)
        slot_of = sb("slot_of", [P, J * E], F32)
        slot_sel = sb("slot_sel", [P, J, 2, E], F32)
        slot_f = sb("slot_f", [P, J * 2], F32)
        slots_g = sb("slots_g", [P, J * 2], U32)
        ids_g = sb("ids_g", [P, J], U32)
        gather_slots = sb("gather_slots", [P, J * 2], U32)
        y_in = sb("y_in", [P, J, 2, D], F32)
        zeros = y_in[:].rearrange("p j k d -> p (j k d)")[:, 0:SP_COLS].bitcast(U32)
        KV = J + RADIUS
        qkv = sb("qkv", [P, KV, 3 * D], F32)
        prod = sb("prod", [P, 2, JC, W, D], F32)
        score = sb("score", [P, J, W, HEADS], F32)
        smax = sb("smax", [P, J, HEADS], F32)
        ssum = sb("ssum", [P, J * HEADS], F32)
        sinv = sb("sinv", [P, J * HEADS], F32)
        counts_i = sb("counts_i", [P, E], I32)
        n_tiles_i = sb("n_tiles_i", [P, E], I32)
        n_tiles = sb("n_tiles", [P, E], F32)
        earlier = sb("earlier", [P, (E + 1) * E], F32)
        plan_t = sb("plan_t", [P, (E + 1) * E], F32)
        tile_start = sb("tile_start", [P, E + 1], F32)
        region = sb("region", [P, E + 1], F32)
        row_off = sb("row_off", [P, E + 1], F32)
        row_jump = sb("row_jump", [P, E], F32)
        tile_no = sb("tile_no", [1, NT], F32)
        tile_expert = sb("tile_expert", [1, NT], I32)
        tile_row = sb("tile_row", [1, NT], I32)
        tile_tok = sb("tile_tok", [P, TOK_RING, 2], U32)
        prod_flat = prod[:].rearrange("p a j w d -> p (a j w d)")
        h_f = prod_flat[:, 0:2 * HC * 256].rearrange("p (a c n) -> p a c n", a=2, c=HC)
        h_hl = prod_flat[:, 2048:2048 + 2048].bitcast(F16).rearrange("p (a s c n) -> p a s c n", a=2, s=2, c=HC)
        xsT = prod_flat[:, 4096:4608].bitcast(F16).rearrange("p (a s i n) -> p a s i n", a=2, s=2, i=2)
        y_sb = prod_flat[:, 4608:5632].rearrange("p (r i d) -> p r i d", r=4, i=2)
        xs = prod_flat[:, 8192:9216].bitcast(F16).rearrange("p (r i c) -> p r i c", r=4, i=2)
        w1_stage = prod_flat[:, 0:E * H]
        w2_stage = prod_flat[:, E * H:2 * E * H]
        qkv_flat = qkv[:].rearrange("p s c -> p (s c)")
        maps4 = qkv_flat[:, 0:NJ * SP_COLS].bitcast(U32).rearrange("p (r n) -> p r n", r=NJ)
        map_sum = qkv_flat[:, NJ * SP_COLS:(NJ + 1) * SP_COLS].bitcast(U32)

        plan_at = (NJ + 1) * SP_COLS
        begun = qkv_flat[0:1, plan_at:plan_at + (E + 2) * NT]
        mine = qkv_flat[0:1, plan_at + (E + 2) * NT:plan_at + (2 * E + 3) * NT]
        mine_w = qkv_flat[0:1, plan_at + (2 * E + 3) * NT:plan_at + (3 * E + 4) * NT]
        map_f = qkv_flat[0:1, plan_at + (3 * E + 4) * NT:plan_at + (3 * E + 6) * NT].rearrange("o (k n) -> o k n", k=2)
        y_row_at = plan_at + (3 * E + 6) * NT
        y_row_f = qkv_flat[:, y_row_at:y_row_at + TILES * 2]
        in_expert = qkv_flat[:, y_row_at + TILES * 2:y_row_at + TILES * 4]
        o_sb = xn
        oT = xnT[:, :, 1:1 + P]

        bank = [ctx.enter_context(nc.psum_tensor(f"bank{i}", [P, 512], F32)) for i in range(6)]
        banks_6_7 = ctx.enter_context(nc.psum_tensor("banks_6_7", [P, 2, 512], F32))
        bank += [banks_6_7[:, 0, :], banks_6_7[:, 1, :]]
        y_banks = banks_6_7[:]

        consts_loaded = sem("consts_loaded")
        w_loaded = sem("w_loaded")
        w_split = sem("w_split")
        x_loaded = sem("x_loaded")
        pool_step = sem("pool_step")
        b1_turned = sem("b1_turned")
        consts_done = sem("consts_done")
        var_ready = sem("var_ready")
        std_ready = sem("std_ready")
        xn_ready = sem("xn_ready")
        xn_turned = sem("xn_turned")
        xnT_ready = sem("xnT_ready")
        logits_ready = sem("logits_ready")
        gate_diff = sem("gate_diff")
        gate_exped = sem("gate_exped")
        chosen_ready = sem("chosen_ready")
        rank_ready = sem("rank_ready")
        hi_ready = sem("hi_ready")
        hl_ready = sem("hl_ready")
        hl_stored = sem("hl_stored")
        slots_ready = sem("slots_ready")
        map_cleared = sems("map_cleared", NJ)
        map_scattered = sems("map_scattered", NJ)
        maps_loaded = sem("maps_loaded")
        maps_added = sem("maps_added")
        map_stored = sem("map_stored")
        plan_ready = sem("plan_ready")
        gather_slots_ready = sem("gather_slots_ready")
        y_gathered = sems("y_gathered", C)
        combined = sem("combined")
        qkv_done = sem("qkv_done")
        qkv_ready = sem("qkv_ready")
        score_ready = sem("score_ready")
        prob_ready = sem("prob_ready")
        pv_ready = sem("pv_ready")
        pv_summed = sem("pv_summed")
        o_ready = sem("o_ready")
        o_turned = sem("o_turned")
        oT_ready = sem("oT_ready")
        attn_done = sem("attn_done")
        attn_added = sem("attn_added")
        out_stored = sem("out_stored")
        tok_loaded = sems("tok_loaded", TOK_RING)
        xs_gathered = sems("xs_gathered", 4)
        xs_turned = sems("xs_turned", 4)
        xsT_ready = sems("xsT_ready", 2)
        h_done = sems("h_done", 2)
        h_gelu = sems("h_gelu", 2)
        h_hi = sems("h_hi", 2)
        h_split = sems("h_split", 2)
        y_done = sem("y_done")
        y_ready = sem("y_ready")
        y_stored = sems("y_stored", 4)
        waits_carried = sem("waits_carried")
        setup_step = sem("setup_step")
        split_step = sem("split_step")
        route_step = sem("route_step")
        group_step = sem("group_step")
        plan_step = sem("plan_step")
        out_step = sem("out_step")

        N_CONSTS = 8

        def xt(t, n=1):
            return x_sb[:, bass.ds(t * D, n * D)]

        def over_expert_tiles(eng, f, step):
            def at(i, first):
                return Tile(i, first, f, NT) if first >= 0 else None
            for k in range(PEEL):
                step(at(0, k), at(0, k + 1), at(0, k - 1), at(0, k - Y_LAG))
            with eng.Fori(0, LOOPS) as i:
                for k in range(PEEL, PEEL + EU):
                    step(at(i, k), at(i, k + 1), at(i, k - 1), at(i, k - Y_LAG))
            for k in range(PEEL + LOOPS * EU, NT):
                step(at(0, k), at(0, k + 1) if k + 1 < NT else None, at(0, k - 1), at(0, k - Y_LAG))

        def carry_waits(eng):
            eng.sem_inc(waits_carried)

        block = ctx.enter_context(nc.Block())

        @block.sync
        def _(sp):
            sp.dma_start(x_sb[:, 0:J * D], x_v[0]).then_inc(x_loaded, DMA)
            for dst, src in ((wg_sb[:], Wg), (bg_bc[:], bg.rearrange("(o e) -> o e", o=1).to_broadcast([P, E])),
                             (b1_rows[:], b1.rearrange("e (c p) -> (e c) p", p=P)),
                             (wqkv[:, 0:D], Wq), (wqkv[:, D:2 * D], Wk), (wqkv[:, 2 * D:], Wv), (wo_sb[:], Wo),
                             (b2_bc[:], b2.rearrange("(o e) d -> o (e d)", o=1).to_broadcast([P, E * D]))):
                sp.dma_start(dst, src).then_inc(consts_loaded, DMA)
            for g in range(1, G):
                sp.wait_ge(x_loaded, g * DMA)
                sp.dma_start(x_sb[:, g * J * D:(g + 1) * J * D], x_v[g]).then_inc(x_loaded, DMA)
            sp.wait_ge(pool_step, 1)
            for r in range(NJ):
                sp.dma_start(slot_token[r].rearrange("(p n) -> p n", p=P), zeros).then_inc(map_cleared[r], DMA)
            sp.dma_start(w1_stage.rearrange("p (e h) -> p e h", e=E), W1.rearrange("e d h -> d e h")).then_inc(w_loaded, DMA)
            sp.dma_start(w2_stage.rearrange("p (e c d) -> p e c d", e=E, c=HC),
                         W2.rearrange("e (c p) d -> p e c d", p=P)).then_inc(w_loaded, DMA)

            def store_hl(q, g):
                sp.wait_ge(hl_ready, q + 1)
                sp.dma_start(x_hl_v[bass.ds(g, 1)].rearrange("a p n -> (a p) n"),
                             hl[:].rearrange("p j c -> p (j c)")).then_inc(hl_stored, DMA)

            def slot_maps(f):
                for r in range(NJ):
                    sp.wait_ge(map_scattered[r], DMA * ((f + 1) * TILES * 2 // NJ))
                    sp.dma_start(maps4[:, r, :], slot_token[r].rearrange("(p n) -> p n", p=P)).then_inc(maps_loaded, DMA)
                sp.wait_ge(maps_added, f + 1)
                sp.dma_start(slot_token_sum.rearrange("(p n) -> p n", p=P), map_sum).then_inc(map_stored, DMA)
                if f == 0:
                    sp.wait_ge(maps_loaded, NJ * DMA)
                    for r in range(NJ):
                        sp.dma_start(slot_token[r].rearrange("(p n) -> p n", p=P), zeros).then_inc(map_cleared[r], DMA)

            def store_y(t):
                sp.wait_ge(y_ready, t.count + 1)
                sp.dma_start(y_rows[bass.ds(t.j * SLOT_TILE, SLOT_TILE), :].rearrange("(p i) d -> p (i d)", i=2),
                              y_sb[:, t.ring].rearrange("p i d -> p (i d)")).then_inc(y_stored[t.ring], DMA)

            def tile_tokens(f):
                sp.wait_ge(plan_ready, f + 1)
                sp.wait_ge(map_stored, (f + 1) * DMA)

                def step(t, nxt, prv, old):
                    row = sp.value_load(tile_row[0:1, bass.ds(t.j, 1)], min_val=0, max_val=SLOTS - SLOT_TILE)
                    sp.dma_start(tile_tok[:, t.tok, :], slot_token_sum[bass.ds(row, SLOT_TILE)]
                                 .rearrange("(p i) -> p i", i=2)).then_inc(tok_loaded[t.tok], DMA)
                    if old:
                        store_y(old)
                over_expert_tiles(sp, f, step)
                for k in range(NT - Y_LAG, NT):
                    store_y(Tile(0, k, f, NT))

            with sp.Fori(0, G) as g:
                store_hl(g, g)
            slot_maps(0)
            tile_tokens(0)
            with sp.Fori(0, G) as g:
                store_hl(g + G, g)
            slot_maps(1)
            tile_tokens(1)
            with sp.Fori(0, G) as g:
                sp.wait_ge(combined, (g + G + 1) * C)
                sp.dma_start(out_v[bass.ds(g, 1)].rearrange("a p n -> (a p) n"),
                             xt(g * J, J)).then_inc(out_stored, DMA)
            sp.wait_ge(out_stored, G * DMA)

        @block.gpsimd
        def _(pool):
            pool.memset(zeros, 0).then_inc(pool_step, 1)
            pool.memset(ident[:], 0.0).then_inc(pool_step, 1)
            pool.memset(ident16[:], 0.0).then_inc(pool_step, 1)
            pool.memset(before16[:], 1.0).then_inc(pool_step, 1)
            pool.memset(window_mask[:], 0.0).then_inc(pool_step, 1)
            pool.memset(earlier[:], 1.0).then_inc(pool_step, 1)
            pool.wait_ge(pool_step, 6)
            pool.affine_select(out=ident[:], in_=ident[:], compare_op=ALU.not_equal, fill=1.0, base=0,
                               pattern=[[-1, P]], channel_multiplier=1).then_inc(pool_step, 1)
            pool.affine_select(out=ident16[:], in_=ident16[:], compare_op=ALU.not_equal, fill=1.0, base=0,
                               pattern=[[-1, P]], channel_multiplier=1).then_inc(pool_step, 1)
            pool.affine_select(out=before16[:], in_=before16[:], compare_op=ALU.is_gt, fill=0.0, base=0,
                               pattern=[[1, P]], channel_multiplier=-1).then_inc(pool_step, 1)
            pool.affine_select(out=window_mask[:].rearrange("p (j w) -> p j w", w=W),
                               in_=window_mask[:].rearrange("p (j w) -> p j w", w=W), compare_op=ALU.is_ge,
                               fill=LOW, base=-RADIUS, pattern=[[1, RADIUS], [1, W]],
                               channel_multiplier=0).then_inc(pool_step, 1)
            pool.affine_select(out=earlier[:].rearrange("o (e f) -> o e f", f=E),
                               in_=earlier[:].rearrange("o (e f) -> o e f", f=E), compare_op=ALU.is_gt,
                               fill=0.0, base=0, pattern=[[1, E + 1], [-1, E]],
                               channel_multiplier=0).then_inc(pool_step, 1)
            pool.iota(e_iota[:].rearrange("p (j e) -> p j e", e=E), [[0, J], [1, E]], base=0,
                      channel_multiplier=0, allow_small_or_imprecise_dtypes=True).then_inc(pool_step, 1)
            pool.iota(token_ids[:].rearrange("p (g j) -> p g j", j=J), [[P * J, G], [1, J]], base=0,
                      channel_multiplier=J).then_inc(pool_step, 1)
            pool.iota(part_i[:], [[0, 1]], base=0, channel_multiplier=1).then_inc(pool_step, 1)
            pool.iota(slot_base[:], [[0, 2], [N, E]], base=0, channel_multiplier=0,
                      allow_small_or_imprecise_dtypes=True).then_inc(pool_step, 1)
            pool.iota(region[:], [[N, E + 1]], base=0, channel_multiplier=0,
                      allow_small_or_imprecise_dtypes=True).then_inc(pool_step, 1)
            pool.iota(tile_no[:], [[1, NT]], base=0, channel_multiplier=0,
                      allow_small_or_imprecise_dtypes=True).then_inc(pool_step, 1)
            pool.memset(ones16[:], 1.0).then_inc(pool_step, 1)
            pool.memset(chosen[:], 0.0).then_inc(pool_step, 1)
            pool.memset(xnT[:], 0.0).then_inc(pool_step, 1)
            pool.memset(y_row[:], 0).then_inc(pool_step, 1)
            pool.wait_ge(pool_step, 21)

            def scatter_ids(q, clears, first=False):
                pool.wait_ge(slots_ready, q + 1)
                for i in range(J * 2):
                    r, m = i % NJ, i // NJ
                    if m > 0 or not first:
                        pool.wait_ge(map_scattered[r], (q * (2 * J // NJ) + m) * DMA)
                    pool.wait_ge(map_cleared[r], clears * DMA)
                    carry_waits(pool)
                    pool.indirect_dma_start(
                        out=slot_token[r].rearrange("(n o) -> n o", o=1),
                        out_offset=bass.IndirectOffsetOnAxis(ap=slots_g[:, i:i + 1], axis=0),
                        in_=ids_g[:, i // 2:i // 2 + 1], in_offset=None).then_inc(map_scattered[r], DMA)

            def gather_y(cr, first, cf):
                pool.wait_ge(gather_slots_ready, cr + (1 + cf))
                for c in range(C):
                    if not first:
                        pool.wait_ge(combined, cr * C + (c + 1 - C))
                    carry_waits(pool)
                    for i in range(c * JC * 2, (c + 1) * JC * 2):
                        pool.indirect_dma_start(
                            out=y_in[:, i // 2, i % 2, :], out_offset=None, in_=y_rows,
                            in_offset=bass.IndirectOffsetOnAxis(ap=gather_slots[:, i:i + 1], axis=0)
                        ).then_inc(y_gathered[c], DMA)

            def gather_tokens(f):
                pool.wait_ge(hl_stored, (f + 1) * G * DMA)

                def step(t, nxt, prv, old):
                    pool.wait_ge(tok_loaded[t.tok], (t.tok_uses + 1) * DMA)
                    if t.ring_reused:
                        pool.wait_ge(xs_turned[t.ring], t.ring_uses)
                    carry_waits(pool)
                    for half in range(2):
                        pool.indirect_dma_start(
                            out=xs[:, t.ring, half, :], out_offset=None, in_=x_hl,
                            in_offset=bass.IndirectOffsetOnAxis(ap=tile_tok[:, t.tok, half:half + 1], axis=0)
                        ).then_inc(xs_gathered[t.ring], DMA)
                over_expert_tiles(pool, f, step)
                for s in range(4):
                    pool.wait_ge(y_stored[s], DMA * (f + 1) * len(range(s, NT, 4)))

            scatter_ids(0, 1, first=True)
            with pool.Fori(1, G) as g:
                scatter_ids(g, 1)
            gather_tokens(0)
            for r in range(NJ):
                pool.wait_ge(map_cleared[r], 2 * DMA)
            gather_y(0, True, 0)
            with pool.Fori(0, G - 1) as g:
                gather_y(g + 1, False, 0)
                scatter_ids(g + G, 2)
            scatter_ids(2 * G - 1, 2)
            gather_tokens(1)
            with pool.Fori(0, G) as g:
                gather_y(g + G, False, 1)

        @block.scalar
        def _(act):
            act.wait_ge(b1_turned, 1)
            act.copy(b1_cols[:], bank[0][:, 0:E * HC]).then_inc(consts_done, 1)

            def norm(r):
                act.wait_ge(var_ready, r + 1)
                act.activation(std[:], var_eps[:], ACT.Sqrt).then_inc(std_ready, 1)
                for c in range(C):
                    act.wait_ge(xn_turned, r * C + (c + 1))
                    act.copy(xnT[:, c * JC:(c + 1) * JC, 1:1 + P],
                             bank[c % 2][:].rearrange("p (j n) -> p j n", n=P)).then_inc(xnT_ready, 1)

            def route(q):
                act.copy(hl[:, :, 0:D], xn[:]).then_inc(hi_ready, 1)
                act.wait_ge(gate_diff, q + 1)
                act.activation(gate_exp[:], gate_exp[:], ACT.Exp).then_inc(gate_exped, 1)
                act.wait_ge(hl_stored, (q + 1) * DMA)

            def attention(g):
                for k in range(KV):
                    act.wait_ge(qkv_done, g * KV + (k + 1))
                    lo = D if k < RADIUS else 0
                    act.copy(qkv[:, k, lo:3 * D], bank[4 + k % 2][:, lo:3 * D]).then_inc(qkv_ready, 1)
                act.wait_ge(score_ready, g + 1)
                act.activation(score[:], score[:], ACT.Exp, scale=SCORE_SCALE).then_inc(prob_ready, 1)
                for c in range(C):
                    act.wait_ge(o_turned, g * C + (c + 1))
                    act.copy(oT[:, c * JC:(c + 1) * JC, :],
                             bank[c % 2][:].rearrange("p (j n) -> p j n", n=P)).then_inc(oT_ready, 1)

            def experts(f):
                act.wait_ge(plan_ready, f + 1)

                def step(t, nxt, prv, old):
                    e = act.value_load(tile_expert[0:1, bass.ds(t.j, 1)], min_val=0, max_val=E - 1)
                    for b in range(2):
                        act.wait_ge(h_done[t.par], t.par_uses * 2 + (b + 1))
                        if t.par_reused:
                            act.wait_ge(h_split[t.par], t.par_uses * 2)
                        for c in (2 * b, 2 * b + 1):
                            ins = act.activation(h_f[:, t.par, c, :], bank[2 + 2 * t.par + b][:, (c % 2) * 256:(c % 2 + 1) * 256],
                                                 ACT.Gelu, bias=b1_cols[:, bass.ds(e * HC + c, 1)], scale=1.0 / WS)
                        ins.then_inc(h_gelu[t.par], 1)
                        act.wait_ge(h_gelu[t.par], t.par_uses * 2 + (b + 1))
                        if t.par_reused:
                            act.wait_ge(y_done, t.count - 1)
                        act.copy(h_hl[:, t.par, 0, 2 * b:2 * b + 2, :],
                                 h_f[:, t.par, 2 * b:2 * b + 2, :]).then_inc(h_hi[t.par], 1)
                over_expert_tiles(act, f, step)

            with act.Fori(0, G) as g:
                norm(g)
                route(g)
            experts(0)
            with act.Fori(0, G) as g:
                norm(g * 2 + G)
                attention(g)
                norm(g * 2 + (G + 1))
                route(g + G)
            experts(1)

        @block.tensor
        def _(pe):
            pe.wait_ge(consts_loaded, N_CONSTS * DMA)
            pe.wait_ge(pool_step, 21)
            pe.transpose(bank[0][:, 0:E * HC], b1_rows[:], ident[0:E * HC, 0:E * HC]).then_inc(b1_turned, 1)
            pe.wait_ge(consts_done, 1)

            def norm(r):
                for c in range(C):
                    pe.wait_ge(xn_ready, r * C + (c + 1))
                    if c >= 2:
                        pe.wait_ge(xnT_ready, r * C + (c - 1))
                    for j in range(JC):
                        ins = pe.transpose(bank[c % 2][:, j * P:(j + 1) * P], xn[:, c * JC + j, :], ident[:])
                    ins.then_inc(xn_turned, 1)

            def route(r, q):
                pe.wait_ge(xnT_ready, r * C + C)
                for j in range(J):
                    ins = pe.matmul(bank[2][:, j * E:(j + 1) * E], xnT[:, j, 1:1 + P], wg_sb[:], start=True, stop=True)
                ins.then_inc(logits_ready, 1)
                pe.wait_ge(chosen_ready, q + 1)
                pe.matmul(bank[3][:, 0:(J + 1) * E], before16[:], chosen[:], start=True, stop=False)
                for j in range(J):
                    ins = pe.matmul(bank[3][:, (j + 1) * E:(J + 1) * E].rearrange("p (n e) -> p n e", e=E), ones16[:],
                                    chosen[:, j * E:(j + 1) * E].rearrange("p (o e) -> p o e", o=1)
                                    .to_broadcast([P, J - j, E]), start=False, stop=(j == J - 1))
                ins.then_inc(rank_ready, 1)

            def attention(g, r):
                pe.wait_ge(xnT_ready, r * C + C)
                for k in range(KV):
                    if k >= 2:
                        pe.wait_ge(qkv_ready, g * KV + (k - 1))
                    if k < RADIUS:
                        pe.matmul(bank[4 + k % 2][:, D:3 * D], xnT[:, J - RADIUS + k, 0:P], wqkv[:, D:3 * D],
                                  start=True, stop=True).then_inc(qkv_done, 1)
                    else:
                        pe.matmul(bank[4 + k % 2][:, 0:3 * D], xnT[:, k - RADIUS, 1:1 + P], wqkv[:],
                                  start=True, stop=True).then_inc(qkv_done, 1)

                def add_window(c):
                    pe.wait_ge(pv_ready, g * C + (c + 1))
                    if c >= 2:
                        pe.wait_ge(o_ready, g * C + (c - 1))
                    for w in range(W):
                        ins = pe.matmul(bank[6 + c % 2][:].rearrange("p (j d) -> p j d", d=D), ident[:],
                                        prod[:, c % 2, :, w, :], start=(w == 0), stop=(w == W - 1))
                    ins.then_inc(pv_summed, 1)

                def turn_o(c):
                    pe.wait_ge(o_ready, g * C + (c + 1))
                    if c >= 2:
                        pe.wait_ge(oT_ready, g * C + (c - 1))
                    for j in range(JC):
                        ins = pe.transpose(bank[c % 2][:, j * P:(j + 1) * P], o_sb[:, c * JC + j, :], ident[:])
                    ins.then_inc(o_turned, 1)

                def project(c):
                    pe.wait_ge(oT_ready, g * C + (c + 1))
                    if c >= 2:
                        pe.wait_ge(attn_added, g * C + (c - 1))
                    for j in range(JC):
                        ins = pe.matmul(bank[4 + c % 2][:, j * D:(j + 1) * D], oT[:, c * JC + j, :], wo_sb[:],
                                        start=True, stop=True)
                    ins.then_inc(attn_done, 1)

                for c in range(C + 2):
                    if c < C:
                        add_window(c)
                    if 1 <= c <= C:
                        turn_o(c - 1)
                    if c >= 2:
                        project(c - 2)

            def experts(f):
                pe.wait_ge(plan_ready, f + 1)
                pe.wait_ge(w_split, 2)

                def turn(t):
                    pe.wait_ge(xs_gathered[t.ring], (t.ring_uses + 1) * 2 * DMA)
                    if t.par_reused:
                        pe.wait_ge(xsT_ready[t.par], t.par_uses)
                    for s in range(2):
                        for half in range(2):
                            at = (2 * s + half) * P
                            ins = pe.transpose(bank[t.par][:].bitcast(F16)[:, at:at + P],
                                               xs[:, t.ring, half, s * D:(s + 1) * D], ident16[:])
                    ins.then_inc(xs_turned[t.ring], 1)

                def expert_of(t):
                    return pe.value_load(tile_expert[0:1, bass.ds(t.j, 1)], min_val=0, max_val=E - 1)

                def up(t, e):
                    pe.wait_ge(xsT_ready[t.par], t.par_uses + 1)
                    if t.par_reused:
                        pe.wait_ge(h_gelu[t.par], t.par_uses * 2)
                    for c in range(HC):
                        dst = bank[2 + 2 * t.par + c // 2][:, (c % 2) * 256:(c % 2 + 1) * 256]
                        for n, (ws, s) in enumerate(((0, 0), (0, 1), (1, 0))):
                            ins = pe.matmul(dst, w1_hl[:, ws, bass.ds(e * H + c * P, P)],
                                            xsT[:, t.par, s].rearrange("p i n -> p (i n)"), start=(n == 0), stop=(n == 2))
                        if c % 2:
                            ins.then_inc(h_done[t.par], 1)

                def down(t, e):
                    pe.wait_ge(h_split[t.par], t.par_uses * 2 + 2)
                    if t.not_first:
                        pe.wait_ge(y_ready, t.count)
                    for c in range(HC):
                        for half in range(2):
                            for n, (s, ws) in enumerate(((0, 0), (0, 1), (1, 0))):
                                ins = pe.matmul(y_banks[:, half, 0:D],
                                                h_hl[:, t.par, s, c, half * P:(half + 1) * P],
                                                w2_hl[:, ws, bass.ds((e * HC + c) * D, D)],
                                                start=(c == 0 and n == 0), stop=(c == HC - 1 and n == 2))
                    ins.then_inc(y_done, 1)

                e_prv = None

                def step(t, nxt, prv, old):
                    nonlocal e_prv
                    if not prv:
                        turn(t)
                    if prv and t.first_of_body:
                        e_prv = expert_of(prv)
                    e = expert_of(t)
                    up(t, e)
                    if nxt:
                        turn(nxt)
                    if prv:
                        down(prv, e_prv)
                    e_prv = e
                over_expert_tiles(pe, f, step)
                down(Tile(0, NT - 1, f, NT), e_prv)

            with pe.Fori(0, G) as g:
                norm(g)
                route(g, g)
            experts(0)
            with pe.Fori(0, G) as g:
                norm(g * 2 + G)
                attention(g, g * 2 + G)
                norm(g * 2 + (G + 1))
                route(g * 2 + (G + 1), g + G)
            experts(1)

        @block.vector
        def _(dve):
            dve.wait_ge(pool_step, 21)
            su = Steps(dve, setup_step, 0)
            su.did(dve.tensor_scalar(part_i[:], part_i[:], LOW_SEQ - 1, None, ALU.bitwise_and))
            su.settle()
            su.did(dve.tensor_scalar(seq_start[:], part_i[:], 0.0, None, ALU.is_equal))
            su.settle()
            su.did(dve.tensor_scalar(window_mask[:], window_mask[:], seq_start[:], None, ALU.mult))
            su.settle()
            dve.wait_ge(consts_loaded, N_CONSTS * DMA)

            def norm(r, t0, st):
                carry_waits(dve)
                for j in range(J):
                    st.did(dve.bn_stats(stats[:, j, :], xt(t0 + j)))
                st.settle()
                carry_waits(dve)
                for j in range(J):
                    st.did(dve.bn_aggr(mean_var[:, j, :], stats[:, j, :]))
                st.settle()
                dve.tensor_scalar(var_eps[:], mean_var[:, :, 1], LN_EPS, None, ALU.add).then_inc(var_ready, 1)
                dve.wait_ge(std_ready, r + 1)
                st.did(dve.reciprocal(rstd[:], std[:]))
                st.settle()
                for c in range(C):
                    for j in range(c * JC, (c + 1) * JC):
                        ins = dve.tensor_scalar(xn[:, j, :], xt(t0 + j), mean_var[:, j, 0:1], rstd[:, j:j + 1],
                                                ALU.subtract, ALU.mult)
                    ins.then_inc(xn_ready, 1)

            def per_e(ap):
                return ap.rearrange("p (j e) -> p j e", e=E)

            def bc_e(ap):
                return ap.rearrange("p (j o) -> p j o", o=1).to_broadcast([P, J, E])

            def route(q, g, st, first=False):
                dve.wait_ge(logits_ready, q + 1)
                st.did(dve.tensor_tensor(per_e(logits[:]), per_e(bank[2][:, 0:J * E]),
                                         bg_bc[:].rearrange("p (o e) -> p o e", o=1).to_broadcast([P, J, E]), ALU.add))
                st.settle()
                for k, source in ((0, logits), (1, logits2)):
                    st.did(dve.tensor_reduce(top[:, k, :], per_e(source[:]), X, ALU.max))
                    st.settle()
                    st.did(dve.tensor_tensor(per_e(cand[:]), per_e(source[:]), bc_e(top[:, k, :]), ALU.not_equal))
                    st.settle()
                    st.did(dve.scalar_tensor_tensor(out=cand2[:], in0=cand[:], scalar=float(E), in1=e_iota[:],
                                                    op0=ALU.mult, op1=ALU.add))
                    st.settle()
                    st.did(dve.tensor_reduce(choice[:, k, :], per_e(cand2[:]), X, ALU.min))
                    st.settle()
                    st.did(dve.tensor_tensor(onehot[:, :, k, :], per_e(e_iota[:]), bc_e(choice[:, k, :]), ALU.is_equal))
                    st.settle()
                    if k == 0:
                        st.did(dve.scalar_tensor_tensor(out=per_e(logits2[:]), in0=onehot[:, :, 0, :], scalar=LOW,
                                                        in1=per_e(logits[:]), op0=ALU.mult, op1=ALU.add))
                        st.settle()
                dve.tensor_tensor(per_e(chosen[:, 0:J * E]), onehot[:, :, 0, :], onehot[:, :, 1, :],
                                  ALU.add).then_inc(chosen_ready, 1)
                st.did(dve.tensor_tensor(gate_exp[:, :, 0:E], per_e(logits[:]), bc_e(top[:, 0, :]), ALU.subtract))
                dve.tensor_tensor(gate_exp[:, :, E], top[:, 1, :], top[:, 0, :], ALU.subtract).then_inc(gate_diff, 1)
                dve.wait_ge(hi_ready, q + 1)
                dve.tensor_tensor(hl[:, :, D:2 * D], xn[:], hl[:, :, 0:D], ALU.subtract).then_inc(hl_ready, 1)
                dve.wait_ge(gate_exped, q + 1)
                st.did(dve.tensor_reduce(gate_sum[:], gate_exp[:, :, 0:E], X, ALU.add))
                st.settle()
                st.did(dve.reciprocal(gate_inv[:], gate_sum[:]))
                st.settle()
                mine2 = gates[:, bass.ds(g * (J * 2), J * 2)].rearrange("p (j k) -> p j k", k=2)
                st.did(dve.tensor_scalar(mine2[:, :, 0], gate_inv[:], 0.5, None, ALU.mult))
                st.did(dve.scalar_tensor_tensor(out=mine2[:, :, 1], in0=gate_exp[:, :, E], scalar=0.5,
                                                in1=gate_inv[:], op0=ALU.mult, op1=ALU.mult))
                dve.wait_ge(rank_ready, q + 1)
                st.did(dve.tensor_tensor(per_e(slot_of[:]), per_e(bank[3][:, 0:J * E]),
                                         slot_base[:, 0, :].rearrange("p (o e) -> p o e", o=1).to_broadcast([P, J, E]),
                                         ALU.add))
                st.settle()
                st.did(dve.tensor_tensor(slot_base[:, 0, :], bank[3][:, J * E:(J + 1) * E], slot_base[:, 0, :], ALU.add))
                st.did(dve.tensor_tensor(slot_sel[:], onehot[:],
                                         slot_of[:].rearrange("p (j o e) -> p j o e", o=1, e=E)
                                         .to_broadcast([P, J, 2, E]), ALU.mult))
                st.settle()
                st.did(dve.tensor_reduce(slot_f[:], slot_sel[:].rearrange("p j k e -> p (j k) e"), X, ALU.add))
                st.settle()
                st.did(dve.tensor_copy(slots_all[:, bass.ds(g * (J * 2), J * 2)], slot_f[:]))
                if not first:
                    for r in range(NJ):
                        dve.wait_ge(map_scattered[r], q * (2 * J // NJ) * DMA)
                st.did(dve.tensor_copy(ids_g[:], token_ids[:, bass.ds(g * J, J)]))
                dve.tensor_copy(slots_g[:], slot_f[:]).then_inc(slots_ready, 1)

            def combine(cr, t0, g2, st):
                for c in range(C):
                    dve.wait_ge(y_gathered[c], (cr + 1) * (2 * JC * DMA))
                    for k in range(2):
                        for j in range(c * JC, (c + 1) * JC):
                            ins = dve.scalar_tensor_tensor(out=xt(t0 + j), in0=y_in[:, j, k, :],
                                                           scalar=gates[:, bass.ds(g2 + (2 * j + k), 1)],
                                                           in1=xt(t0 + j), op0=ALU.mult, op1=ALU.add)
                            if k == 0:
                                st.did(ins)
                        if k == 0:
                            st.settle()
                    ins.then_inc(combined, 1)

            def next_gather(g2):
                dve.tensor_copy(gather_slots[:], y_row[:, bass.ds(g2, J * 2)]).then_inc(gather_slots_ready, 1)

            def attention(g, st):
                for c in range(C):
                    dve.wait_ge(qkv_ready, g * KV + (RADIUS + (c + 1) * JC))
                    lo = c * JC
                    pc = prod[:, c % 2]
                    q_ap = qkv[:, RADIUS + lo:RADIUS + lo + JC, 0:D].rearrange("p j (o d) -> p j o d", o=1)
                    st.did(dve.tensor_tensor(pc, q_ap.to_broadcast([P, JC, W, D]), windows(lo, D), ALU.mult))
                    st.settle()
                    st.did(dve.tensor_reduce(score[:, lo:lo + JC].rearrange("p j w h -> p (j w h)"),
                                             pc.rearrange("p j w (h d) -> p (j w h) d", d=DK), X, ALU.add))
                st.settle()
                first = score[:, 0:RADIUS].rearrange("p j w h -> p (j w) h")
                st.did(dve.tensor_tensor(first, first, window_mask[:].rearrange("p (n o) -> p n o", o=1)
                                         .to_broadcast([P, RADIUS * W, HEADS]), ALU.add))
                st.settle()
                st.did(dve.tensor_reduce(smax[:], score[:].rearrange("p j w h -> p j h w"), X, ALU.max))
                st.settle()
                dve.tensor_tensor(score[:], score[:], smax[:].rearrange("p j (o h) -> p j o h", o=1)
                                  .to_broadcast([P, J, W, HEADS]), ALU.subtract).then_inc(score_ready, 1)
                dve.wait_ge(prob_ready, g + 1)

                def prob_value(c):
                    lo = c * JC
                    if c >= 2:
                        dve.wait_ge(pv_summed, g * C + (c - 1))
                    dve.tensor_tensor(prod[:, c % 2].rearrange("p j w (h d) -> p j w h d", d=DK),
                                      score[:, lo:lo + JC].rearrange("p j w (h o) -> p j w h o", o=1)
                                      .to_broadcast([P, JC, W, HEADS, DK]),
                                      windows(lo, 2 * D, heads=True), ALU.mult).then_inc(pv_ready, 1)

                def take_o(c):
                    dve.wait_ge(pv_summed, g * C + (c + 1))
                    n = JC * HEADS
                    dve.tensor_tensor(o_sb[:, c * JC:(c + 1) * JC, :].rearrange("p j (h d) -> p (j h) d", d=DK),
                                      bank[6 + c % 2][:].rearrange("p (n d) -> p n d", d=DK),
                                      sinv[:, c * n:(c + 1) * n].rearrange("p (n o) -> p n o", o=1)
                                      .to_broadcast([P, n, DK]), ALU.mult).then_inc(o_ready, 1)

                def add_attention(c):
                    dve.wait_ge(attn_done, g * C + (c + 1))
                    here = xt(g * J + c * JC, JC)
                    dve.tensor_tensor(here, bank[4 + c % 2][:], here, ALU.add).then_inc(attn_added, 1)

                prob_value(0)
                prob_value(1)
                st.did(dve.tensor_reduce(ssum[:].rearrange("p (j h) -> p j h", h=HEADS),
                                         score[:].rearrange("p j w h -> p j h w"), X, ALU.add))
                st.settle()
                st.did(dve.reciprocal(sinv[:], ssum[:]))
                st.settle()
                for c in range(C):
                    take_o(c)
                    if c + 2 < C:
                        prob_value(c + 2)
                for c in range(C):
                    add_attention(c)
                dve.wait_ge(attn_added, g * C + C)

            def windows(lo, at, heads=False):
                a = qkv[:, lo:lo + 1, at:at + D]
                inner = [[DK, HEADS], [1, DK]] if heads else [[1, D]]
                return bass.AP(a.tensor, a.offset, [list(a.ap[0]), [3 * D, JC], [3 * D, W]] + inner)

            def split_weights():
                st = Steps(dve, split_step, 0)
                dve.wait_ge(w_loaded, 2 * DMA)
                for stage, pair in ((w1_stage, w1_hl), (w2_stage, w2_hl)):
                    st.did(dve.tensor_scalar(pair[:, 0, :], stage, WS, None, ALU.mult))
                    st.settle()
                    dve.scalar_tensor_tensor(out=pair[:, 1, :], in0=stage, scalar=WS, in1=pair[:, 0, :],
                                             op0=ALU.mult, op1=ALU.subtract).then_inc(w_split, 1)

            def plan(f):
                st = Steps(dve, plan_step, f * PLAN_STEPS)
                def did(ins):
                    st.did(ins)
                    st.settle()
                e1 = E + 1
                did(dve.tensor_tensor(plan_t[:, 0:E], slot_base[:, 0, :], region[:, 0:E], ALU.subtract))
                did(dve.tensor_scalar(counts_i[:], plan_t[:, 0:E], float(SLOT_TILE - 1), None, ALU.add))
                did(dve.tensor_scalar(n_tiles_i[:], counts_i[:], SLOT_TILE.bit_length() - 1, None, ALU.logical_shift_right))
                did(dve.tensor_copy(n_tiles[:], n_tiles_i[:]))
                did(dve.tensor_tensor(plan_t[:].rearrange("o (e f) -> o e f", f=E),
                                      earlier[:].rearrange("o (e f) -> o e f", f=E),
                                      n_tiles[:].rearrange("o (e f) -> o e f", e=1).to_broadcast([P, e1, E]), ALU.mult))
                did(dve.tensor_reduce(tile_start[:], plan_t[:].rearrange("o (e f) -> o e f", f=E), X, ALU.add))
                did(dve.scalar_tensor_tensor(out=row_off[:], in0=tile_start[:], scalar=-float(SLOT_TILE),
                                             in1=region[:], op0=ALU.mult, op1=ALU.add))
                tiles_bc = tile_no[:].rearrange("o (e n) -> o e n", e=1).to_broadcast([1, e1, NT])
                did(dve.memset(begun[:, e1 * NT:], 0.0))
                did(dve.tensor_tensor(begun[:, 0:e1 * NT].rearrange("o (e n) -> o e n", n=NT), tiles_bc,
                                      tile_start[0:1, :].rearrange("o (e n) -> o e n", n=1).to_broadcast([1, e1, NT]), ALU.is_ge))
                did(dve.tensor_tensor(mine[:], begun[:, 0:e1 * NT], begun[:, NT:], ALU.subtract))
                mine_v = mine[:].rearrange("o (e n) -> o e n", n=NT)
                mine_wv = mine_w[:].rearrange("o (e n) -> o e n", n=NT)
                did(dve.tensor_tensor(mine_wv, mine_v, row_off[0:1, :].rearrange("o (e n) -> o e n", n=1)
                                      .to_broadcast([1, e1, NT]), ALU.mult))
                did(dve.tensor_reduce(map_f[:, 0, :], mine_w[:].rearrange("o (e n) -> o n e", n=NT), X, ALU.add))
                did(dve.scalar_tensor_tensor(out=tile_row[:], in0=tile_no[:], scalar=float(SLOT_TILE),
                                             in1=map_f[:, 0, :], op0=ALU.mult, op1=ALU.add))
                did(dve.tensor_reduce(map_f[:, 1, :], begun[:, NT:E * NT].rearrange("o (e n) -> o n e", n=NT), X, ALU.add))
                dve.tensor_copy(tile_expert[:], map_f[:, 1, :]).then_inc(plan_ready, 1)
                dve.wait_ge(maps_loaded, (f + 1) * NJ * DMA)
                did(dve.tensor_tensor(map_sum, maps4[:, 0, :], maps4[:, 1, :], ALU.bitwise_or))
                did(dve.tensor_tensor(map_sum, map_sum, maps4[:, 2, :], ALU.bitwise_or))
                dve.tensor_tensor(map_sum, map_sum, maps4[:, 3, :], ALU.bitwise_or).then_inc(maps_added, 1)
                did(dve.tensor_tensor(row_jump[:], row_off[:, 1:], row_off[:, 0:E], ALU.subtract))
                for e in range(1, E):
                    did(dve.tensor_scalar(in_expert, slots_all[:], float(e * N), row_jump[:, e - 1:e], ALU.is_ge, ALU.mult))
                    did(dve.tensor_tensor(y_row_f, y_row_f if e > 1 else slots_all[:], in_expert, ALU.subtract))
                did(dve.tensor_copy(y_row[:, 0:TILES * 2], y_row_f))
                if f == 0:
                    did(dve.tensor_copy(slot_base[:, 0, :], slot_base[:, 1, :]))
                assert st.n == PLAN_STEPS - f, st.n + f

            def experts(f):
                last = Tile(0, NT - 1, f, NT)

                def copy_xT(t):
                    dve.wait_ge(xs_turned[t.ring], t.ring_uses + 1)
                    if t.par_reused:
                        dve.wait_ge(h_done[t.par], t.par_uses * 2)
                    dve.tensor_copy(xsT[:, t.par].rearrange("p s i n -> p (s i n)"),
                                    bank[t.par][:].bitcast(F16)[:, 0:4 * P]).then_inc(xsT_ready[t.par], 1)

                def split_h(t, b):
                    dve.wait_ge(h_hi[t.par], t.par_uses * 2 + (b + 1))
                    dve.tensor_tensor(h_hl[:, t.par, 1, 2 * b:2 * b + 2, :], h_f[:, t.par, 2 * b:2 * b + 2, :],
                                      h_hl[:, t.par, 0, 2 * b:2 * b + 2, :], ALU.subtract).then_inc(h_split[t.par], 1)

                def take_y(t, e):
                    dve.wait_ge(y_done, t.count + 1)
                    if t.ring_reused:
                        dve.wait_ge(y_stored[t.ring], t.ring_uses * DMA)
                    dve.scalar_tensor_tensor(
                        out=y_sb[:, t.ring], in0=y_banks[:, :, 0:D],
                        scalar=1.0 / WS, in1=b2_bc[:, bass.ds(e * D, D)].rearrange("p (o d) -> p o d", o=1)
                        .to_broadcast([P, 2, D]), op0=ALU.mult, op1=ALU.add).then_inc(y_ready, 1)

                def step(t, nxt, prv, old):
                    if not prv:
                        copy_xT(t)
                    if prv:
                        e = dve.value_load(tile_expert[0:1, bass.ds(prv.j, 1)], min_val=0, max_val=E - 1)
                    if nxt:
                        copy_xT(nxt)
                    split_h(t, 0)
                    if prv:
                        take_y(prv, e)
                    split_h(t, 1)
                over_expert_tiles(dve, f, step)
                take_y(last, dve.value_load(tile_expert[0:1, bass.ds(last.j, 1)], min_val=0, max_val=E - 1))

            def first_pass(g, first):
                st = Steps(dve, route_step, g * ROUTE_STEPS)
                dve.wait_ge(x_loaded, (g + 1) * DMA)
                norm(g, g * J, st)
                route(g, g, st, first)
                assert st.n == ROUTE_STEPS, st.n

            first_pass(0, True)
            with dve.Fori(1, G) as g:
                first_pass(g, False)
            split_weights()
            plan(0)
            experts(0)
            next_gather(0)
            with dve.Fori(0, G) as g:
                st = Steps(dve, group_step, g * GROUP_STEPS)
                combine(g, g * J, g * (J * 2), st)
                next_gather(g * (J * 2) + J * 2)
                dve.wait_ge(combined, g * C + C)
                norm(g * 2 + G, g * J, st)
                attention(g, st)
                norm(g * 2 + (G + 1), g * J, st)
                route(g + G, g, st)
                assert st.n == GROUP_STEPS, st.n
            plan(1)
            experts(1)
            next_gather(0)
            with dve.Fori(0, G) as g:
                st = Steps(dve, out_step, g * (2 * J // 2))
                combine(g + G, g * J, g * (J * 2), st)
                next_gather(g * (J * 2) + J * 2)


_INS = ["L0_attn_x", "L0_attn_Wq", "L0_attn_Wk", "L0_attn_Wv", "L0_attn_Wo", "L0_ffn_Wg", "L0_ffn_bg",
        "L0_ffn_W1", "L0_ffn_b1", "L0_ffn_W2", "L0_ffn_b2"]


def kernel(**inputs):
    import numpy as _np
    import concourse.bacc as _bacc
    from concourse import mybir as _mybir
    from concourse.bass_utils import run_bass_kernel_spmd as _run

    nc = _bacc.Bacc("TRN2", target_bir_lowering=False, num_devices=1)
    arrays, args = {}, []
    for name in _INS:
        a = _np.ascontiguousarray(inputs[name])
        arrays[f"in_{name}"] = a
        args.append(nc.dram_tensor(f"in_{name}", a.shape, _mybir.dt.from_np(a.dtype), kind="ExternalInput").ap())
    args.append(nc.dram_tensor("out_0", arrays["in_L0_attn_x"].shape, F32, kind="ExternalOutput").ap())
    macaron(nc, *args)
    r = _run(nc, [arrays], core_ids=[0])
    return r.results[0]["out_0"]
```

```python
from contextlib import ExitStack

import concourse.bass as bass
from concourse import mybir

F32 = mybir.dt.float32
F16 = mybir.dt.float16
BF16 = mybir.dt.bfloat16
I32 = mybir.dt.int32
U32 = mybir.dt.uint32
ALU = mybir.AluOpType
ACT = mybir.ActivationFunctionType
X = mybir.AxisListType.X

P = 128
D = 128
E = 8
H = 512
HC = H // P
HEADS = 16
DK = D // HEADS
RADIUS = 8
W = RADIUS + 1
SCORE_SCALE = 1.0 / (2.0 * 0.28)
LN_EPS = 1e-5
WS = 64.0
LOW = -1e30
J = 16
C = 4
JC = J // C
SLOT_TILE = 256
NJ = 4
SPARE = 12
EU = 16
PEEL = 6
Y_LAG = 6
TOK_RING = 8
ROUTE_STEPS = 56
GROUP_STEPS = 120
PLAN_STEPS = 33
VALUES_HALF = (1, 1, 0, 1)
DMA = 16


class Steps:

    def __init__(self, eng, sem, before):
        self.eng, self.sem, self.before, self.n = eng, sem, before, 0

    def did(self, ins):
        ins.then_inc(self.sem, 1)
        self.n += 1

    def settle(self):
        if self.n:
            self.eng.wait_ge(self.sem, self.before + self.n)


class Tile:

    def __init__(self, i, first, f, n_tiles):
        def uses(n):
            return i * (EU // n) + (first // n + f * len(range(first % n, n_tiles, n)))
        self.j = i * EU + first
        self.ring, self.ring_uses = first % 4, uses(4)
        self.par, self.par_uses = first % 2, uses(2)
        self.tok, self.tok_uses = first % TOK_RING, uses(TOK_RING)
        self.first_of_body = not isinstance(i, int) and first == PEEL or isinstance(i, int) and first > PEEL and (first - PEEL) % EU == 0
        self.count = i * EU + (first + f * n_tiles)
        self.not_first = f > 0 or first > 0
        self.ring_reused = f > 0 or first >= 4
        self.par_reused = f > 0 or first >= 2


def macaron(nc, x, Wq, Wk, Wv, Wo, Wg, bg, W1, b1, W2, b2, out):
    B, S, _ = x.shape
    N = B * S
    G = N // (P * J)
    TILES = G * J
    NT = (2 * N - E) // SLOT_TILE + E
    LOOPS = (NT - PEEL - 1) // EU
    SLOTS = E * N + SPARE * SLOT_TILE
    SP_COLS = SLOTS // P
    LOW_SEQ = S // J

    x_hl = nc.dram_tensor("x_hl", [N, 2 * D], F16, kind="Internal").ap()
    slot_token = [nc.dram_tensor(f"slot_token{r}", [SLOTS], U32, kind="Internal").ap() for r in range(NJ)]
    slot_token_sum = nc.dram_tensor("slot_token_sum", [SLOTS], U32, kind="Internal").ap()
    y_rows = nc.dram_tensor("y_rows", [NT * SLOT_TILE, D], F32, kind="Internal").ap()

    x_v = x.flatten_outer_dims().rearrange("(g p j) d -> g p (j d)", p=P, j=J)
    out_v = out.flatten_outer_dims().rearrange("(g p j) d -> g p (j d)", p=P, j=J)
    x_hl_v = x_hl.rearrange("(g p j) c -> g p (j c)", p=P, j=J)

    with ExitStack() as ctx:
        def sb(name, shape, dt):
            return ctx.enter_context(nc.sbuf_tensor(name, shape, dt))

        def sem(name):
            return ctx.enter_context(nc.semaphore(name))

        def sems(name, n):
            return [sem(f"{name}{i}") for i in range(n)]

        x_sb = sb("x_sb", [P, TILES * D], F32)
        w1_hl = sb("w1_hl", [P, 2, E * H], F16)
        w2_hl = sb("w2_hl", [P, E * HC, 2, D], F16)
        wqkv = sb("wqkv", [P, 3 * D], F32)
        wo_sb = sb("wo_sb", [P, D], F32)
        wg_sb = sb("wg_sb", [P, E], F32)
        bg_bc = sb("bg_bc", [P, E], F32)
        b1_rows = sb("b1_rows", [E * HC, P], F32)
        b1_cols = sb("b1_cols", [P, E * HC], F32)
        b2_bc = sb("b2_bc", [P, E * D], F32)
        ident = sb("ident", [P, P], F32)
        ident16 = sb("ident16", [P, P], F16)
        before16 = sb("before16", [P, P], BF16)
        ones16 = sb("ones16", [P, P], BF16)
        e_iota = sb("e_iota", [P, J * E], F32)
        token_ids = sb("token_ids", [P, TILES], U32)
        window_mask = sb("window_mask", [P, RADIUS * W], F32)
        part_i = sb("part_i", [P, 1], I32)
        seq_start = sb("seq_start", [P, 1], F32)
        gates = sb("gates", [P, TILES * 2], F32)
        slots_all = sb("slots_all", [P, TILES * 2], F32)
        y_row = sb("y_row", [P, (TILES + J) * 2], U32)
        stats = sb("stats", [P, J, 6], F32)
        mean_var = sb("mean_var", [P, J, 2], F32)
        var_eps = sb("var_eps", [P, 2, J], F32)
        std = sb("std", [P, 2, J], F32)
        rstd = sb("rstd", [P, 2, J], F32)
        xn = sb("xn", [P, J, D], F32)
        xnT = sb("xnT", [P, J, D + 2], F32)
        hl = sb("hl", [P, J, 2 * D], F16)
        logits = sb("logits", [P, J * E], F32)
        top = sb("top", [P, 2, J], F32)
        cand = sb("cand", [P, J * E], F32)
        cand2 = sb("cand2", [P, J * E], F32)
        choice = sb("choice", [P, 2, J], F32)
        onehot = sb("onehot", [P, J, 2, E], F32)
        logits2 = sb("logits2", [P, J * E], F32)
        gate_exp = sb("gate_exp", [P, J, E + 1], F32)
        gate_sum = sb("gate_sum", [P, J], F32)
        gate_inv = sb("gate_inv", [P, J], F32)
        chosen = sb("chosen", [P, (J + 1) * E], BF16)
        slot_base = sb("slot_base", [P, 2, E], F32)
        slot_of = sb("slot_of", [P, J * E], F32)
        slot_sel = sb("slot_sel", [P, J, 2, E], F32)
        slot_f = sb("slot_f", [P, J * 2], F32)
        slots_g = sb("slots_g", [P, J * 2], U32)
        ids_g = sb("ids_g", [P, J], U32)
        gather_slots = sb("gather_slots", [P, J * 2], U32)
        y_in = sb("y_in", [P, J, 2, D], F32)
        zeros = y_in[:].rearrange("p j k d -> p (j k d)")[:, 0:SP_COLS].bitcast(U32)
        KV = J + RADIUS
        qkv = sb("qkv", [P, KV, 3 * D], F32)
        prod = sb("prod", [P, 2, JC, W, D], F32)
        score = sb("score", [P, J, W, HEADS], F32)
        smax = sb("smax", [P, J // 2, HEADS], F32)
        ssum = sb("ssum", [P, J * HEADS], F32)
        sinv = sb("sinv", [P, J * HEADS], F32)
        counts_i = sb("counts_i", [P, E], I32)
        n_tiles_i = sb("n_tiles_i", [P, E], I32)
        n_tiles = sb("n_tiles", [P, E], F32)
        earlier = sb("earlier", [P, (E + 1) * E], F32)
        plan_t = sb("plan_t", [P, (E + 1) * E], F32)
        tile_start = sb("tile_start", [P, E + 1], F32)
        region = sb("region", [P, E + 1], F32)
        row_off = sb("row_off", [P, E + 1], F32)
        row_jump = sb("row_jump", [P, E], F32)
        tile_no = sb("tile_no", [1, NT], F32)
        tile_expert = sb("tile_expert", [1, NT], I32)
        tile_row = sb("tile_row", [1, NT], I32)
        tile_tok = sb("tile_tok", [P, TOK_RING, 2], U32)
        prod_flat = prod[:].rearrange("p a j w d -> p (a j w d)")
        h_f = prod_flat[:, 0:2 * HC * 256].rearrange("p (a c n) -> p a c n", a=2, c=HC)
        h_hl = prod_flat[:, 2048:2048 + 2048].bitcast(F16).rearrange("p (a s c n) -> p a s c n", a=2, s=2, c=HC)
        xsT = prod_flat[:, 4096:4608].bitcast(F16).rearrange("p (a s i n) -> p a s i n", a=2, s=2, i=2)
        y_sb = prod_flat[:, 4608:5632].rearrange("p (r i d) -> p r i d", r=4, i=2)
        xs = prod_flat[:, 8192:9216].bitcast(F16).rearrange("p (r i c) -> p r i c", r=4, i=2)
        w1_stage = prod_flat[:, 0:E * H]
        w2_stage = prod_flat[:, E * H:2 * E * H]
        qkv_flat = qkv[:].rearrange("p s c -> p (s c)")
        maps4 = qkv_flat[:, 0:NJ * SP_COLS].bitcast(U32).rearrange("p (r n) -> p r n", r=NJ)
        map_sum = qkv_flat[:, NJ * SP_COLS:(NJ + 1) * SP_COLS].bitcast(U32)

        plan_at = (NJ + 1) * SP_COLS
        begun = qkv_flat[0:1, plan_at:plan_at + (E + 2) * NT]
        mine = qkv_flat[0:1, plan_at + (E + 2) * NT:plan_at + (2 * E + 3) * NT]
        mine_w = qkv_flat[0:1, plan_at + (2 * E + 3) * NT:plan_at + (3 * E + 4) * NT]
        map_f = qkv_flat[0:1, plan_at + (3 * E + 4) * NT:plan_at + (3 * E + 6) * NT].rearrange("o (k n) -> o k n", k=2)
        y_row_at = plan_at + (3 * E + 6) * NT
        y_row_f = qkv_flat[:, y_row_at:y_row_at + TILES * 2]
        in_expert = qkv_flat[:, y_row_at + TILES * 2:y_row_at + TILES * 4]
        o_sb = xn
        oT = xnT[:, :, 1:1 + P]

        banks_0_1 = ctx.enter_context(nc.psum_tensor("banks_0_1", [P, 2, 512], F32))
        bank = [banks_0_1[:, 0, :], banks_0_1[:, 1, :]]
        bank += [ctx.enter_context(nc.psum_tensor(f"bank{i}", [P, 512], F32)) for i in range(2, 6)]
        banks_6_7 = ctx.enter_context(nc.psum_tensor("banks_6_7", [P, 2, 512], F32))
        bank += [banks_6_7[:, 0, :], banks_6_7[:, 1, :]]
        y_banks = banks_6_7[:]
        score_banks = banks_0_1[:, :, 0:JC // 2 * W * HEADS]

        consts_loaded = sem("consts_loaded")
        w_loaded = sem("w_loaded")
        w_split = sem("w_split")
        x_loaded = sem("x_loaded")
        pool_step = sem("pool_step")
        b1_turned = sem("b1_turned")
        consts_done = sem("consts_done")
        var_ready = sem("var_ready")
        std_ready = sem("std_ready")
        xn_ready = sem("xn_ready")
        xn_turned = sem("xn_turned")
        xnT_ready = sem("xnT_ready")
        logits_ready = sem("logits_ready")
        gate_diff = sem("gate_diff")
        gate_exped = sem("gate_exped")
        chosen_ready = sem("chosen_ready")
        rank_ready = sem("rank_ready")
        hi_ready = sem("hi_ready")
        hl_ready = sem("hl_ready")
        hl_stored = sem("hl_stored")
        slots_ready = sem("slots_ready")
        map_cleared = sems("map_cleared", NJ)
        map_scattered = sems("map_scattered", NJ)
        maps_loaded = sem("maps_loaded")
        maps_added = sem("maps_added")
        map_stored = sem("map_stored")
        plan_ready = sem("plan_ready")
        gather_slots_ready = sem("gather_slots_ready")
        y_gathered = sems("y_gathered", C)
        combined = sem("combined")
        qkv_done = sem("qkv_done")
        qkv_ready = sem("qkv_ready")
        keys_multiplied = sem("keys_multiplied")
        channels_added = sem("channels_added")
        score_ready = sem("score_ready")
        prob_ready = sem("prob_ready")
        pv_ready = sem("pv_ready")
        pv_summed = sem("pv_summed")
        o_ready = sem("o_ready")
        o_turned = sem("o_turned")
        oT_ready = sem("oT_ready")
        attn_done = sem("attn_done")
        attn_added = sem("attn_added")
        out_stored = sem("out_stored")
        tok_loaded = sems("tok_loaded", TOK_RING)
        xs_gathered = sems("xs_gathered", 4)
        xs_turned = sems("xs_turned", 4)
        xsT_ready = sems("xsT_ready", 2)
        h_done = sems("h_done", 2)
        h_gelu = sems("h_gelu", 2)
        h_hi = sems("h_hi", 2)
        h_split = sems("h_split", 2)
        y_done = sem("y_done")
        y_begun = sem("y_begun")
        y_ready = sem("y_ready")
        y_stored = sems("y_stored", 4)
        waits_carried = sem("waits_carried")
        setup_step = sem("setup_step")
        split_step = sem("split_step")
        route_step = sem("route_step")
        group_step = sem("group_step")
        plan_step = sem("plan_step")
        out_step = sem("out_step")

        N_CONSTS = 8

        def xt(t, n=1):
            return x_sb[:, bass.ds(t * D, n * D)]

        def over_expert_tiles(eng, f, step):
            def at(i, first):
                return Tile(i, first, f, NT) if first >= 0 else None
            for k in range(PEEL):
                step(at(0, k), at(0, k + 1), at(0, k - 1), at(0, k - Y_LAG))
            with eng.Fori(0, LOOPS) as i:
                for k in range(PEEL, PEEL + EU):
                    step(at(i, k), at(i, k + 1), at(i, k - 1), at(i, k - Y_LAG))
            for k in range(PEEL + LOOPS * EU, NT):
                step(at(0, k), at(0, k + 1) if k + 1 < NT else None, at(0, k - 1), at(0, k - Y_LAG))

        def carry_waits(eng):
            eng.sem_inc(waits_carried)

        block = ctx.enter_context(nc.Block())

        @block.sync
        def _(sp):
            sp.dma_start(x_sb[:, 0:J * D], x_v[0]).then_inc(x_loaded, DMA)
            for dst, src in ((wg_sb[:], Wg), (bg_bc[:], bg.rearrange("(o e) -> o e", o=1).to_broadcast([P, E])),
                             (b1_rows[:], b1.rearrange("e (c p) -> (e c) p", p=P)),
                             (wqkv[:, 0:D], Wq), (wqkv[:, D:2 * D], Wk), (wqkv[:, 2 * D:], Wv), (wo_sb[:], Wo),
                             (b2_bc[:], b2.rearrange("(o e) d -> o (e d)", o=1).to_broadcast([P, E * D]))):
                sp.dma_start(dst, src).then_inc(consts_loaded, DMA)
            for g in range(1, G):
                sp.wait_ge(x_loaded, g * DMA)
                sp.dma_start(x_sb[:, g * J * D:(g + 1) * J * D], x_v[g]).then_inc(x_loaded, DMA)
            sp.wait_ge(pool_step, 1)
            for r in range(NJ):
                sp.dma_start(slot_token[r].rearrange("(p n) -> p n", p=P), zeros).then_inc(map_cleared[r], DMA)
            sp.dma_start(w1_stage.rearrange("p (e h) -> p e h", e=E), W1.rearrange("e d h -> d e h")).then_inc(w_loaded, DMA)
            sp.dma_start(w2_stage.rearrange("p (e c d) -> p e c d", e=E, c=HC),
                         W2.rearrange("e (c p) d -> p e c d", p=P)).then_inc(w_loaded, DMA)

            def store_hl(q, g):
                sp.wait_ge(hl_ready, q + 1)
                sp.dma_start(x_hl_v[bass.ds(g, 1)].rearrange("a p n -> (a p) n"),
                             hl[:].rearrange("p j c -> p (j c)")).then_inc(hl_stored, DMA)

            def slot_maps(f):
                for r in range(NJ):
                    sp.wait_ge(map_scattered[r], DMA * ((f + 1) * TILES * 2 // NJ))
                    sp.dma_start(maps4[:, r, :], slot_token[r].rearrange("(p n) -> p n", p=P)).then_inc(maps_loaded, DMA)
                sp.wait_ge(maps_added, f + 1)
                sp.dma_start(slot_token_sum.rearrange("(p n) -> p n", p=P), map_sum).then_inc(map_stored, DMA)
                if f == 0:
                    sp.wait_ge(maps_loaded, NJ * DMA)
                    for r in range(NJ):
                        sp.dma_start(slot_token[r].rearrange("(p n) -> p n", p=P), zeros).then_inc(map_cleared[r], DMA)

            def store_y(t):
                sp.wait_ge(y_ready, t.count + 1)
                sp.dma_start(y_rows[bass.ds(t.j * SLOT_TILE, SLOT_TILE), :].rearrange("(p i) d -> p (i d)", i=2),
                              y_sb[:, t.ring].rearrange("p i d -> p (i d)")).then_inc(y_stored[t.ring], DMA)

            def tile_tokens(f):
                sp.wait_ge(plan_ready, f + 1)
                sp.wait_ge(map_stored, (f + 1) * DMA)

                def step(t, nxt, prv, old):
                    row = sp.value_load(tile_row[0:1, bass.ds(t.j, 1)], min_val=0, max_val=SLOTS - SLOT_TILE)
                    sp.dma_start(tile_tok[:, t.tok, :], slot_token_sum[bass.ds(row, SLOT_TILE)]
                                 .rearrange("(p i) -> p i", i=2)).then_inc(tok_loaded[t.tok], DMA)
                    if old:
                        store_y(old)
                over_expert_tiles(sp, f, step)
                for k in range(NT - Y_LAG, NT):
                    store_y(Tile(0, k, f, NT))

            with sp.Fori(0, G) as g:
                store_hl(g, g)
            slot_maps(0)
            tile_tokens(0)
            with sp.Fori(0, G) as g:
                store_hl(g + G, g)
            slot_maps(1)
            tile_tokens(1)
            with sp.Fori(0, G) as g:
                sp.wait_ge(combined, (g + G + 1) * C)
                sp.dma_start(out_v[bass.ds(g, 1)].rearrange("a p n -> (a p) n"),
                             xt(g * J, J)).then_inc(out_stored, DMA)
            sp.wait_ge(out_stored, G * DMA)

        @block.gpsimd
        def _(pool):
            pool.memset(zeros, 0).then_inc(pool_step, 1)
            pool.memset(ident[:], 0.0).then_inc(pool_step, 1)
            pool.memset(ident16[:], 0.0).then_inc(pool_step, 1)
            pool.memset(before16[:], 1.0).then_inc(pool_step, 1)
            pool.memset(window_mask[:], 0.0).then_inc(pool_step, 1)
            pool.memset(earlier[:], 1.0).then_inc(pool_step, 1)
            pool.wait_ge(pool_step, 6)
            pool.affine_select(out=ident[:], in_=ident[:], compare_op=ALU.not_equal, fill=1.0, base=0,
                               pattern=[[-1, P]], channel_multiplier=1).then_inc(pool_step, 1)
            pool.affine_select(out=ident16[:], in_=ident16[:], compare_op=ALU.not_equal, fill=1.0, base=0,
                               pattern=[[-1, P]], channel_multiplier=1).then_inc(pool_step, 1)
            pool.affine_select(out=before16[:], in_=before16[:], compare_op=ALU.is_gt, fill=0.0, base=0,
                               pattern=[[1, P]], channel_multiplier=-1).then_inc(pool_step, 1)
            pool.affine_select(out=window_mask[:].rearrange("p (j w) -> p j w", w=W),
                               in_=window_mask[:].rearrange("p (j w) -> p j w", w=W), compare_op=ALU.is_ge,
                               fill=LOW, base=-RADIUS, pattern=[[1, RADIUS], [1, W]],
                               channel_multiplier=0).then_inc(pool_step, 1)
            pool.affine_select(out=earlier[:].rearrange("o (e f) -> o e f", f=E),
                               in_=earlier[:].rearrange("o (e f) -> o e f", f=E), compare_op=ALU.is_gt,
                               fill=0.0, base=0, pattern=[[1, E + 1], [-1, E]],
                               channel_multiplier=0).then_inc(pool_step, 1)
            pool.iota(e_iota[:].rearrange("p (j e) -> p j e", e=E), [[0, J], [1, E]], base=0,
                      channel_multiplier=0, allow_small_or_imprecise_dtypes=True).then_inc(pool_step, 1)
            pool.iota(token_ids[:].rearrange("p (g j) -> p g j", j=J), [[P * J, G], [1, J]], base=0,
                      channel_multiplier=J).then_inc(pool_step, 1)
            pool.iota(part_i[:], [[0, 1]], base=0, channel_multiplier=1).then_inc(pool_step, 1)
            pool.iota(slot_base[:], [[0, 2], [N, E]], base=0, channel_multiplier=0,
                      allow_small_or_imprecise_dtypes=True).then_inc(pool_step, 1)
            pool.iota(region[:], [[N, E + 1]], base=0, channel_multiplier=0,
                      allow_small_or_imprecise_dtypes=True).then_inc(pool_step, 1)
            pool.iota(tile_no[:], [[1, NT]], base=0, channel_multiplier=0,
                      allow_small_or_imprecise_dtypes=True).then_inc(pool_step, 1)
            pool.memset(ones16[:], 1.0).then_inc(pool_step, 1)
            pool.memset(chosen[:], 0.0).then_inc(pool_step, 1)
            pool.memset(xnT[:], 0.0).then_inc(pool_step, 1)
            pool.memset(y_row[:], 0).then_inc(pool_step, 1)
            pool.wait_ge(pool_step, 21)

            def scatter_ids(q, clears, first=False):
                pool.wait_ge(slots_ready, q + 1)
                for i in range(J * 2):
                    r, m = i % NJ, i // NJ
                    if m > 0 or not first:
                        pool.wait_ge(map_scattered[r], (q * (2 * J // NJ) + m) * DMA)
                    pool.wait_ge(map_cleared[r], clears * DMA)
                    carry_waits(pool)
                    pool.indirect_dma_start(
                        out=slot_token[r].rearrange("(n o) -> n o", o=1),
                        out_offset=bass.IndirectOffsetOnAxis(ap=slots_g[:, i:i + 1], axis=0),
                        in_=ids_g[:, i // 2:i // 2 + 1], in_offset=None).then_inc(map_scattered[r], DMA)

            def gather_y(cr, first, cf):
                pool.wait_ge(gather_slots_ready, cr + (1 + cf))
                for c in range(C):
                    if not first:
                        pool.wait_ge(combined, cr * C + (c + 1 - C))
                    carry_waits(pool)
                    for i in range(c * JC * 2, (c + 1) * JC * 2):
                        pool.indirect_dma_start(
                            out=y_in[:, i // 2, i % 2, :], out_offset=None, in_=y_rows,
                            in_offset=bass.IndirectOffsetOnAxis(ap=gather_slots[:, i:i + 1], axis=0)
                        ).then_inc(y_gathered[c], DMA)

            def gather_tokens(f):
                pool.wait_ge(hl_stored, (f + 1) * G * DMA)

                def step(t, nxt, prv, old):
                    pool.wait_ge(tok_loaded[t.tok], (t.tok_uses + 1) * DMA)
                    if t.ring_reused:
                        pool.wait_ge(xs_turned[t.ring], t.ring_uses)
                    carry_waits(pool)
                    for half in range(2):
                        pool.indirect_dma_start(
                            out=xs[:, t.ring, half, :], out_offset=None, in_=x_hl,
                            in_offset=bass.IndirectOffsetOnAxis(ap=tile_tok[:, t.tok, half:half + 1], axis=0)
                        ).then_inc(xs_gathered[t.ring], DMA)
                over_expert_tiles(pool, f, step)
                for s in range(4):
                    pool.wait_ge(y_stored[s], DMA * (f + 1) * len(range(s, NT, 4)))

            scatter_ids(0, 1, first=True)
            with pool.Fori(1, G) as g:
                scatter_ids(g, 1)
            gather_tokens(0)
            for r in range(NJ):
                pool.wait_ge(map_cleared[r], 2 * DMA)
            gather_y(0, True, 0)
            gather_y(1, False, 0)
            with pool.Fori(0, G - 2) as g:
                gather_y(g + 2, False, 0)
                scatter_ids(g + G, 2)
            scatter_ids(2 * G - 2, 2)
            scatter_ids(2 * G - 1, 2)
            gather_tokens(1)
            with pool.Fori(0, G) as g:
                gather_y(g + G, False, 1)

        @block.scalar
        def _(act):
            act.wait_ge(b1_turned, 1)
            act.copy(b1_cols[:], bank[0][:, 0:E * HC]).then_inc(consts_done, 1)

            def sqrt(v, kind):
                act.wait_ge(var_ready, v + 1)
                act.activation(std[:, kind, :], var_eps[:, kind, :], ACT.Sqrt).then_inc(std_ready, 1)

            def copy_xnT(r):
                for c in range(C):
                    act.wait_ge(xn_turned, r * C + (c + 1))
                    act.copy(xnT[:, c * JC:(c + 1) * JC, 1:1 + P],
                             bank[c % 2][:].rearrange("p (j n) -> p j n", n=P)).then_inc(xnT_ready, 1)

            def copy_hi(r):
                act.wait_ge(xn_ready, r * C + C)
                act.copy(hl[:, :, 0:D], xn[:]).then_inc(hi_ready, 1)

            def gate_exponentials(q):
                act.wait_ge(gate_diff, q + 1)
                act.activation(gate_exp[:], gate_exp[:], ACT.Exp).then_inc(gate_exped, 1)

            def copy_qkv(g, between=None):
                for k in range(KV):
                    if k == RADIUS and between:
                        between()
                    act.wait_ge(qkv_done, g * KV + (k + 1))
                    lo = D if k < RADIUS else 0
                    act.copy(qkv[:, k, lo:3 * D], bank[4 + k % 2][:, lo:3 * D]).then_inc(qkv_ready, 1)

            def attention(g):
                for h in range(2):
                    mine = score[:, h * J // 2:(h + 1) * J // 2]
                    act.wait_ge(score_ready, g * 2 + (h + 1))
                    act.activation(mine, mine, ACT.Exp, scale=SCORE_SCALE).then_inc(prob_ready, 1)
                for c in range(C):
                    act.wait_ge(o_turned, g * C + (c + 1))
                    act.copy(oT[:, c * JC:(c + 1) * JC, :],
                             bank[c % 2][:].rearrange("p (j n) -> p j n", n=P)).then_inc(oT_ready, 1)

            def experts(f):
                act.wait_ge(plan_ready, f + 1)

                def step(t, nxt, prv, old):
                    e = act.value_load(tile_expert[0:1, bass.ds(t.j, 1)], min_val=0, max_val=E - 1)
                    for b in range(2):
                        act.wait_ge(h_done[t.par], t.par_uses * 2 + (b + 1))
                        if t.par_reused:
                            act.wait_ge(h_split[t.par], t.par_uses * 2)
                        for c in (2 * b, 2 * b + 1):
                            ins = act.activation(h_f[:, t.par, c, :], bank[2 + 2 * t.par + b][:, (c % 2) * 256:(c % 2 + 1) * 256],
                                                 ACT.Gelu, bias=b1_cols[:, bass.ds(e * HC + c, 1)], scale=1.0 / WS)
                        ins.then_inc(h_gelu[t.par], 1)
                        act.wait_ge(h_gelu[t.par], t.par_uses * 2 + (b + 1))
                        if t.par_reused:
                            act.wait_ge(y_done, t.count - 1)
                        act.copy(h_hl[:, t.par, 0, 2 * b:2 * b + 2, :],
                                 h_f[:, t.par, 2 * b:2 * b + 2, :]).then_inc(h_hi[t.par], 1)
                over_expert_tiles(act, f, step)

            with act.Fori(0, G) as g:
                sqrt(g, 0)
                copy_xnT(g)
                copy_hi(g)
                gate_exponentials(g)
                act.wait_ge(hl_stored, (g + 1) * DMA)
            experts(0)

            def second_pass(g, last):
                attention(g)
                sqrt(g * 2 + (G + 1), 0)
                copy_xnT(g * 2 + (G + 1))
                act.wait_ge(hl_stored, (g + G) * DMA)
                copy_hi(g * 2 + (G + 1))
                if last:
                    gate_exponentials(g + G)
                else:
                    sqrt(g * 2 + (G + 2), 1)
                    act.wait_ge(logits_ready, g + (G + 1))
                    copy_xnT(g * 2 + (G + 2))
                    copy_qkv(g + 1, lambda: gate_exponentials(g + G))

            sqrt(G, 1)
            copy_xnT(G)
            copy_qkv(0)
            with act.Fori(0, G - 1) as g:
                second_pass(g, False)
            second_pass(G - 1, True)
            experts(1)

        @block.tensor
        def _(pe):
            pe.wait_ge(consts_loaded, N_CONSTS * DMA)
            pe.wait_ge(pool_step, 21)
            pe.transpose(bank[0][:, 0:E * HC], b1_rows[:], ident[0:E * HC, 0:E * HC]).then_inc(b1_turned, 1)
            pe.wait_ge(consts_done, 1)

            def norm(r, route_logits=False):
                for c in range(C + 1):
                    if c < C:
                        pe.wait_ge(xn_ready, r * C + (c + 1))
                        if c >= 2:
                            pe.wait_ge(xnT_ready, r * C + (c - 1))
                        for j in range(JC):
                            ins = pe.transpose(bank[c % 2][:, j * P:(j + 1) * P], xn[:, c * JC + j, :], ident[:])
                        ins.then_inc(xn_turned, 1)
                    if c > 0 and route_logits:
                        pe.wait_ge(xnT_ready, r * C + c)
                        for j in range((c - 1) * JC, c * JC):
                            ins = pe.matmul(bank[2][:, j * E:(j + 1) * E], xnT[:, j, 1:1 + P], wg_sb[:],
                                            start=True, stop=True)
                if route_logits:
                    ins.then_inc(logits_ready, 1)

            def rank(q):
                pe.wait_ge(chosen_ready, q + 1)
                pe.matmul(bank[3][:, 0:(J + 1) * E], before16[:], chosen[:], start=True, stop=False)
                for j in range(J):
                    ins = pe.matmul(bank[3][:, (j + 1) * E:(J + 1) * E].rearrange("p (n e) -> p n e", e=E), ones16[:],
                                    chosen[:, j * E:(j + 1) * E].rearrange("p (o e) -> p o e", o=1)
                                    .to_broadcast([P, J - j, E]), start=False, stop=(j == J - 1))
                ins.then_inc(rank_ready, 1)

            def make_qkv(g, r, between=None):
                pe.wait_ge(xnT_ready, r * C + C)
                for k in range(KV):
                    if k == RADIUS and between:
                        between()
                    if k >= 2:
                        pe.wait_ge(qkv_ready, g * KV + (k - 1))
                    if k < RADIUS:
                        pe.matmul(bank[4 + k % 2][:, D:3 * D], xnT[:, J - RADIUS + k, 0:P], wqkv[:, D:3 * D],
                                  start=True, stop=True).then_inc(qkv_done, 1)
                    else:
                        pe.matmul(bank[4 + k % 2][:, 0:3 * D], xnT[:, k - RADIUS, 1:1 + P], wqkv[:],
                                  start=True, stop=True).then_inc(qkv_done, 1)

            def attention(g):
                pe.wait_ge(keys_multiplied, g + 1)
                products = prod[:, 1].rearrange("p (a j) w (h d) -> p a (j w h) d", a=2, d=DK)
                for half in range(2):
                    for d in range(DK):
                        ins = pe.matmul(score_banks[:, half, :], ident[:], products[:, half, :, d],
                                        start=(d == 0), stop=(d == DK - 1))
                ins.then_inc(channels_added, 1)

                def add_window(c):
                    pe.wait_ge(pv_ready, g * C + (c + 1))
                    if c >= 2:
                        pe.wait_ge(o_ready, g * C + (c - 1))
                    for w in range(W):
                        ins = pe.matmul(bank[6 + c % 2][:].rearrange("p (j d) -> p j d", d=D), ident[:],
                                        prod[:, VALUES_HALF[c], :, w, :], start=(w == 0), stop=(w == W - 1))
                    ins.then_inc(pv_summed, 1)

                def turn_o(c):
                    pe.wait_ge(o_ready, g * C + (c + 1))
                    if c >= 2:
                        pe.wait_ge(oT_ready, g * C + (c - 1))
                    for j in range(JC):
                        ins = pe.transpose(bank[c % 2][:, j * P:(j + 1) * P], o_sb[:, c * JC + j, :], ident[:])
                    ins.then_inc(o_turned, 1)

                def project(c):
                    pe.wait_ge(oT_ready, g * C + (c + 1))
                    if c >= 2:
                        pe.wait_ge(attn_added, g * C + (c - 1))
                    for j in range(JC):
                        ins = pe.matmul(bank[4 + c % 2][:, j * D:(j + 1) * D], oT[:, c * JC + j, :], wo_sb[:],
                                        start=True, stop=True)
                    ins.then_inc(attn_done, 1)

                for c in range(C + 2):
                    if c < C:
                        add_window(c)
                    if 1 <= c <= C:
                        turn_o(c - 1)
                    if c >= 2:
                        project(c - 2)

            def experts(f):
                pe.wait_ge(plan_ready, f + 1)
                pe.wait_ge(w_split, 2)

                def turn(t):
                    pe.wait_ge(xs_gathered[t.ring], (t.ring_uses + 1) * 2 * DMA)
                    if t.par_reused:
                        pe.wait_ge(xsT_ready[t.par], t.par_uses)
                    for s in range(2):
                        for half in range(2):
                            at = (2 * s + half) * P
                            ins = pe.transpose(bank[t.par][:].bitcast(F16)[:, at:at + P],
                                               xs[:, t.ring, half, s * D:(s + 1) * D], ident16[:])
                    ins.then_inc(xs_turned[t.ring], 1)

                def expert_of(t):
                    return pe.value_load(tile_expert[0:1, bass.ds(t.j, 1)], min_val=0, max_val=E - 1)

                def up(t, e):
                    pe.wait_ge(xsT_ready[t.par], t.par_uses + 1)
                    if t.par_reused:
                        pe.wait_ge(h_gelu[t.par], t.par_uses * 2)
                    for c in range(HC):
                        dst = bank[2 + 2 * t.par + c // 2][:, (c % 2) * 256:(c % 2 + 1) * 256]
                        for n, (ws, s) in enumerate(((0, 0), (0, 1), (1, 0))):
                            ins = pe.matmul(dst, w1_hl[:, ws, bass.ds(e * H + c * P, P)],
                                            xsT[:, t.par, s].rearrange("p i n -> p (i n)"), start=(n == 0), stop=(n == 2))
                        if c % 2:
                            ins.then_inc(h_done[t.par], 1)

                w2_flat = w2_hl[:].rearrange("p n s d -> p (n s d)")

                def down(t, e):
                    if t.not_first:
                        pe.wait_ge(y_ready, t.count)
                    for c in range(HC):
                        if c % 2 == 0:
                            pe.wait_ge(h_split[t.par], t.par_uses * 2 + (c // 2 + 1))
                        at = (e * HC + c) * (2 * D)
                        for half in range(2):
                            pe.matmul(y_banks[:, half, 0:2 * D], h_hl[:, t.par, 0, c, half * P:(half + 1) * P],
                                      w2_flat[:, bass.ds(at, 2 * D)], start=(c == 0), stop=False)
                            ins = pe.matmul(y_banks[:, half, 0:D], h_hl[:, t.par, 1, c, half * P:(half + 1) * P],
                                            w2_flat[:, bass.ds(at, D)], start=False, stop=(c == HC - 1))
                    ins.then_inc(y_done, 1)

                e_prv = None

                def step(t, nxt, prv, old):
                    nonlocal e_prv
                    if not prv:
                        turn(t)
                    if prv and t.first_of_body:
                        e_prv = expert_of(prv)
                    e = expert_of(t)
                    up(t, e)
                    if nxt:
                        turn(nxt)
                    if prv:
                        down(prv, e_prv)
                    e_prv = e
                over_expert_tiles(pe, f, step)
                down(Tile(0, NT - 1, f, NT), e_prv)

            with pe.Fori(0, G) as g:
                norm(g, route_logits=True)
                rank(g)
            experts(0)
            norm(G)
            make_qkv(0, G)
            with pe.Fori(0, G - 1) as g:
                attention(g)
                norm(g * 2 + (G + 1), route_logits=True)
                norm(g * 2 + (G + 2))
                make_qkv(g + 1, g * 2 + (G + 2), lambda: rank(g + G))
            attention(G - 1)
            norm(3 * G - 1, route_logits=True)
            rank(2 * G - 1)
            experts(1)

        @block.vector
        def _(dve):
            dve.wait_ge(pool_step, 21)
            su = Steps(dve, setup_step, 0)
            su.did(dve.tensor_scalar(part_i[:], part_i[:], LOW_SEQ - 1, None, ALU.bitwise_and))
            su.settle()
            su.did(dve.tensor_scalar(seq_start[:], part_i[:], 0.0, None, ALU.is_equal))
            su.settle()
            su.did(dve.tensor_scalar(window_mask[:], window_mask[:], seq_start[:], None, ALU.mult))
            su.settle()
            dve.wait_ge(consts_loaded, N_CONSTS * DMA)

            def statistics(t0, kind, st):
                carry_waits(dve)
                for j in range(J):
                    st.did(dve.bn_stats(stats[:, j, :], xt(t0 + j)))
                st.settle()
                carry_waits(dve)
                for j in range(J):
                    st.did(dve.bn_aggr(mean_var[:, j, :], stats[:, j, :]))
                st.settle()
                dve.tensor_scalar(var_eps[:, kind, :], mean_var[:, :, 1], LN_EPS, None, ALU.add).then_inc(var_ready, 1)

            def norm(r, t0, kind, st):
                dve.wait_ge(std_ready, r + 1)
                st.did(dve.reciprocal(rstd[:, kind, :], std[:, kind, :]))
                st.settle()
                for c in range(C):
                    for j in range(c * JC, (c + 1) * JC):
                        ins = dve.tensor_scalar(xn[:, j, :], xt(t0 + j), mean_var[:, j, 0:1], rstd[:, kind, j:j + 1],
                                                ALU.subtract, ALU.mult)
                    ins.then_inc(xn_ready, 1)

            def per_e(ap):
                return ap.rearrange("p (j e) -> p j e", e=E)

            def bc_e(ap):
                return ap.rearrange("p (j o) -> p j o", o=1).to_broadcast([P, J, E])

            def low_halves(q):
                dve.wait_ge(hi_ready, q + 1)
                dve.tensor_tensor(hl[:, :, D:2 * D], xn[:], hl[:, :, 0:D], ALU.subtract).then_inc(hl_ready, 1)

            def route(q, g, st, first=False):
                dve.wait_ge(logits_ready, q + 1)
                st.did(dve.tensor_tensor(per_e(logits[:]), per_e(bank[2][:, 0:J * E]),
                                         bg_bc[:].rearrange("p (o e) -> p o e", o=1).to_broadcast([P, J, E]), ALU.add))
                st.settle()
                for k, source in ((0, logits), (1, logits2)):
                    st.did(dve.tensor_reduce(top[:, k, :], per_e(source[:]), X, ALU.max))
                    st.settle()
                    st.did(dve.tensor_tensor(per_e(cand[:]), per_e(source[:]), bc_e(top[:, k, :]), ALU.not_equal))
                    st.settle()
                    st.did(dve.scalar_tensor_tensor(out=cand2[:], in0=cand[:], scalar=float(E), in1=e_iota[:],
                                                    op0=ALU.mult, op1=ALU.add))
                    st.settle()
                    st.did(dve.tensor_reduce(choice[:, k, :], per_e(cand2[:]), X, ALU.min))
                    st.settle()
                    st.did(dve.tensor_tensor(onehot[:, :, k, :], per_e(e_iota[:]), bc_e(choice[:, k, :]), ALU.is_equal))
                    st.settle()
                    if k == 0:
                        st.did(dve.scalar_tensor_tensor(out=per_e(logits2[:]), in0=onehot[:, :, 0, :], scalar=LOW,
                                                        in1=per_e(logits[:]), op0=ALU.mult, op1=ALU.add))
                        st.settle()
                dve.tensor_tensor(per_e(chosen[:, 0:J * E]), onehot[:, :, 0, :], onehot[:, :, 1, :],
                                  ALU.add).then_inc(chosen_ready, 1)
                st.did(dve.tensor_tensor(gate_exp[:, :, 0:E], per_e(logits[:]), bc_e(top[:, 0, :]), ALU.subtract))
                dve.tensor_tensor(gate_exp[:, :, E], top[:, 1, :], top[:, 0, :], ALU.subtract).then_inc(gate_diff, 1)
                dve.wait_ge(rank_ready, q + 1)
                st.did(dve.tensor_tensor(per_e(slot_of[:]), per_e(bank[3][:, 0:J * E]),
                                         slot_base[:, 0, :].rearrange("p (o e) -> p o e", o=1).to_broadcast([P, J, E]),
                                         ALU.add))
                st.settle()
                st.did(dve.tensor_tensor(slot_base[:, 0, :], bank[3][:, J * E:(J + 1) * E], slot_base[:, 0, :], ALU.add))
                st.did(dve.tensor_tensor(slot_sel[:], onehot[:],
                                         slot_of[:].rearrange("p (j o e) -> p j o e", o=1, e=E)
                                         .to_broadcast([P, J, 2, E]), ALU.mult))
                st.settle()
                st.did(dve.tensor_reduce(slot_f[:], slot_sel[:].rearrange("p j k e -> p (j k) e"), X, ALU.add))
                st.settle()
                st.did(dve.tensor_copy(slots_all[:, bass.ds(g * (J * 2), J * 2)], slot_f[:]))
                if not first:
                    for r in range(NJ):
                        dve.wait_ge(map_scattered[r], q * (2 * J // NJ) * DMA)
                st.did(dve.tensor_copy(ids_g[:], token_ids[:, bass.ds(g * J, J)]))
                dve.tensor_copy(slots_g[:], slot_f[:]).then_inc(slots_ready, 1)
                dve.wait_ge(gate_exped, q + 1)
                st.did(dve.tensor_reduce(gate_sum[:], gate_exp[:, :, 0:E], X, ALU.add))
                st.settle()
                st.did(dve.reciprocal(gate_inv[:], gate_sum[:]))
                st.settle()
                mine2 = gates[:, bass.ds(g * (J * 2), J * 2)].rearrange("p (j k) -> p j k", k=2)
                st.did(dve.tensor_scalar(mine2[:, :, 0], gate_inv[:], 0.5, None, ALU.mult))
                st.did(dve.scalar_tensor_tensor(out=mine2[:, :, 1], in0=gate_exp[:, :, E], scalar=0.5,
                                                in1=gate_inv[:], op0=ALU.mult, op1=ALU.mult))

            def combine(cr, t0, g2, st, chunks=range(C)):
                for c in chunks:
                    dve.wait_ge(y_gathered[c], (cr + 1) * (2 * JC * DMA))
                    for k in range(2):
                        for j in range(c * JC, (c + 1) * JC):
                            ins = dve.scalar_tensor_tensor(out=xt(t0 + j), in0=y_in[:, j, k, :],
                                                           scalar=gates[:, bass.ds(g2 + (2 * j + k), 1)],
                                                           in1=xt(t0 + j), op0=ALU.mult, op1=ALU.add)
                            if k == 0:
                                st.did(ins)
                        if k == 0:
                            st.settle()
                    ins.then_inc(combined, 1)

            def next_gather(g2):
                dve.tensor_copy(gather_slots[:], y_row[:, bass.ds(g2, J * 2)]).then_inc(gather_slots_ready, 1)

            def attention(g, st, last):
                HJ = J // 2
                keys_half = (0, 1, 0, 0)

                def multiply_keys(c):
                    lo = c * JC
                    dve.wait_ge(qkv_ready, g * KV + (RADIUS + (c + 1) * JC))
                    st.settle()
                    q_ap = qkv[:, RADIUS + lo:RADIUS + lo + JC, 0:D].rearrange("p j (o d) -> p j o d", o=1)
                    ins = dve.tensor_tensor(prod[:, keys_half[c]], q_ap.to_broadcast([P, JC, W, D]),
                                            windows(lo, D), ALU.mult)
                    if c == 1:
                        ins.then_inc(keys_multiplied, 1)
                    else:
                        st.did(ins)

                def add_channels(c):
                    st.settle()
                    st.did(dve.tensor_reduce(score[:, c * JC:(c + 1) * JC].rearrange("p j w h -> p (j w h)"),
                                             prod[:, keys_half[c]].rearrange("p j w (h d) -> p (j w h) d", d=DK), X, ALU.add))

                def subtract_max(h):
                    mine = score[:, h * HJ:(h + 1) * HJ]
                    st.settle()
                    if h == 0:
                        n = JC * W
                        first = mine[:, 0:JC].rearrange("p j w h -> p (j w) h")
                        st.did(dve.tensor_tensor(first, first, window_mask[:, 0:n].rearrange("p (n o) -> p n o", o=1)
                                                 .to_broadcast([P, n, HEADS]), ALU.add))
                        dve.wait_ge(channels_added, g + 1)
                        for a in range(2):
                            second = mine[:, JC + a * JC // 2:JC + (a + 1) * JC // 2]
                            mask = window_mask[:, n + a * n // 2:n + (a + 1) * n // 2]
                            st.did(dve.tensor_tensor(second.rearrange("p j w h -> p (j w) h"),
                                                     score_banks[:, a, :].rearrange("p (n h) -> p n h", h=HEADS),
                                                     mask.rearrange("p (n o) -> p n o", o=1)
                                                     .to_broadcast([P, n // 2, HEADS]), ALU.add))
                        st.settle()
                    st.did(dve.tensor_reduce(smax[:], mine.rearrange("p j w h -> p j h w"), X, ALU.max))
                    st.settle()
                    dve.tensor_tensor(mine, mine, smax[:].rearrange("p j (o h) -> p j o h", o=1)
                                      .to_broadcast([P, HJ, W, HEADS]), ALU.subtract).then_inc(score_ready, 1)

                def prob_value(c):
                    lo = c * JC
                    dve.wait_ge(prob_ready, g * 2 + (c // 2 + 1))
                    st.settle()
                    if c % 2:
                        dve.wait_ge(pv_summed, g * C + {1: 1, 3: 2}[c])
                    dve.tensor_tensor(prod[:, VALUES_HALF[c]].rearrange("p j w (h d) -> p j w h d", d=DK),
                                      score[:, lo:lo + JC].rearrange("p j w (h o) -> p j w h o", o=1)
                                      .to_broadcast([P, JC, W, HEADS, DK]),
                                      windows(lo, 2 * D, heads=True), ALU.mult).then_inc(pv_ready, 1)

                def add_probs(h):
                    n = HJ * HEADS
                    st.did(dve.tensor_reduce(ssum[:, h * n:(h + 1) * n].rearrange("p (j h) -> p j h", h=HEADS),
                                             score[:, h * HJ:(h + 1) * HJ].rearrange("p j w h -> p j h w"), X, ALU.add))
                    st.settle()
                    st.did(dve.reciprocal(sinv[:, h * n:(h + 1) * n], ssum[:, h * n:(h + 1) * n]))
                    st.settle()

                def take_o(c):
                    dve.wait_ge(pv_summed, g * C + (c + 1))
                    n = JC * HEADS
                    dve.tensor_tensor(o_sb[:, c * JC:(c + 1) * JC, :].rearrange("p j (h d) -> p (j h) d", d=DK),
                                      bank[6 + c % 2].rearrange("p (n d) -> p n d", d=DK),
                                      sinv[:, c * n:(c + 1) * n].rearrange("p (n o) -> p n o", o=1)
                                      .to_broadcast([P, n, DK]), ALU.mult).then_inc(o_ready, 1)

                def add_attention(c):
                    dve.wait_ge(attn_done, g * C + (c + 1))
                    here = xt(g * J + c * JC, JC)
                    dve.tensor_tensor(here, bank[4 + c % 2][:], here, ALU.add).then_inc(attn_added, 1)

                multiply_keys(0)
                add_channels(0)
                multiply_keys(1)
                multiply_keys(2)
                add_channels(2)
                subtract_max(0)
                prob_value(0)
                multiply_keys(3)
                add_channels(3)
                prob_value(1)
                subtract_max(1)
                add_probs(0)
                take_o(0)
                prob_value(2)
                take_o(1)
                prob_value(3)
                add_probs(1)
                if not last:
                    combine(g + 1, (g + 1) * J, (g + 1) * (J * 2), st, range(0, 2))
                take_o(2)
                if not last:
                    combine(g + 1, (g + 1) * J, (g + 1) * (J * 2), st, range(2, C))
                take_o(3)
                if not last:
                    next_gather((g + 2) * (J * 2))
                for c in range(C):
                    add_attention(c)
                dve.wait_ge(attn_added, g * C + C)

            def windows(lo, at, heads=False):
                a = qkv[:, lo:lo + 1, at:at + D]
                inner = [[DK, HEADS], [1, DK]] if heads else [[1, D]]
                return bass.AP(a.tensor, a.offset, [list(a.ap[0]), [3 * D, JC], [3 * D, W]] + inner)

            def split_weights():
                st = Steps(dve, split_step, 0)
                dve.wait_ge(w_loaded, 2 * DMA)
                for stage, hi, lo in ((w1_stage, w1_hl[:, 0, :], w1_hl[:, 1, :]),
                                      (w2_stage.rearrange("p (n d) -> p n d", d=D), w2_hl[:, :, 0, :], w2_hl[:, :, 1, :])):
                    st.did(dve.tensor_scalar(hi, stage, WS, None, ALU.mult))
                    st.settle()
                    dve.scalar_tensor_tensor(out=lo, in0=stage, scalar=WS, in1=hi,
                                             op0=ALU.mult, op1=ALU.subtract).then_inc(w_split, 1)

            def plan(f):
                st = Steps(dve, plan_step, f * PLAN_STEPS)
                def did(ins):
                    st.did(ins)
                    st.settle()
                e1 = E + 1
                did(dve.tensor_tensor(plan_t[:, 0:E], slot_base[:, 0, :], region[:, 0:E], ALU.subtract))
                did(dve.tensor_scalar(counts_i[:], plan_t[:, 0:E], float(SLOT_TILE - 1), None, ALU.add))
                did(dve.tensor_scalar(n_tiles_i[:], counts_i[:], SLOT_TILE.bit_length() - 1, None, ALU.logical_shift_right))
                did(dve.tensor_copy(n_tiles[:], n_tiles_i[:]))
                did(dve.tensor_tensor(plan_t[:].rearrange("o (e f) -> o e f", f=E),
                                      earlier[:].rearrange("o (e f) -> o e f", f=E),
                                      n_tiles[:].rearrange("o (e f) -> o e f", e=1).to_broadcast([P, e1, E]), ALU.mult))
                did(dve.tensor_reduce(tile_start[:], plan_t[:].rearrange("o (e f) -> o e f", f=E), X, ALU.add))
                did(dve.scalar_tensor_tensor(out=row_off[:], in0=tile_start[:], scalar=-float(SLOT_TILE),
                                             in1=region[:], op0=ALU.mult, op1=ALU.add))
                tiles_bc = tile_no[:].rearrange("o (e n) -> o e n", e=1).to_broadcast([1, e1, NT])
                did(dve.memset(begun[:, e1 * NT:], 0.0))
                did(dve.tensor_tensor(begun[:, 0:e1 * NT].rearrange("o (e n) -> o e n", n=NT), tiles_bc,
                                      tile_start[0:1, :].rearrange("o (e n) -> o e n", n=1).to_broadcast([1, e1, NT]), ALU.is_ge))
                did(dve.tensor_tensor(mine[:], begun[:, 0:e1 * NT], begun[:, NT:], ALU.subtract))
                mine_v = mine[:].rearrange("o (e n) -> o e n", n=NT)
                mine_wv = mine_w[:].rearrange("o (e n) -> o e n", n=NT)
                did(dve.tensor_tensor(mine_wv, mine_v, row_off[0:1, :].rearrange("o (e n) -> o e n", n=1)
                                      .to_broadcast([1, e1, NT]), ALU.mult))
                did(dve.tensor_reduce(map_f[:, 0, :], mine_w[:].rearrange("o (e n) -> o n e", n=NT), X, ALU.add))
                did(dve.scalar_tensor_tensor(out=tile_row[:], in0=tile_no[:], scalar=float(SLOT_TILE),
                                             in1=map_f[:, 0, :], op0=ALU.mult, op1=ALU.add))
                did(dve.tensor_reduce(map_f[:, 1, :], begun[:, NT:E * NT].rearrange("o (e n) -> o n e", n=NT), X, ALU.add))
                dve.tensor_copy(tile_expert[:], map_f[:, 1, :]).then_inc(plan_ready, 1)
                dve.wait_ge(maps_loaded, (f + 1) * NJ * DMA)
                did(dve.tensor_tensor(map_sum, maps4[:, 0, :], maps4[:, 1, :], ALU.bitwise_or))
                did(dve.tensor_tensor(map_sum, map_sum, maps4[:, 2, :], ALU.bitwise_or))
                dve.tensor_tensor(map_sum, map_sum, maps4[:, 3, :], ALU.bitwise_or).then_inc(maps_added, 1)
                did(dve.tensor_tensor(row_jump[:], row_off[:, 1:], row_off[:, 0:E], ALU.subtract))
                for e in range(1, E):
                    did(dve.tensor_scalar(in_expert, slots_all[:], float(e * N), row_jump[:, e - 1:e], ALU.is_ge, ALU.mult))
                    did(dve.tensor_tensor(y_row_f, y_row_f if e > 1 else slots_all[:], in_expert, ALU.subtract))
                did(dve.tensor_copy(y_row[:, 0:TILES * 2], y_row_f))
                if f == 0:
                    did(dve.tensor_copy(slot_base[:, 0, :], slot_base[:, 1, :]))
                assert st.n == PLAN_STEPS - f, st.n + f

            def experts(f):
                last = Tile(0, NT - 1, f, NT)

                def copy_xT(t):
                    dve.wait_ge(xs_turned[t.ring], t.ring_uses + 1)
                    if t.par_reused:
                        dve.wait_ge(h_done[t.par], t.par_uses * 2)
                    dve.tensor_copy(xsT[:, t.par].rearrange("p s i n -> p (s i n)"),
                                    bank[t.par][:].bitcast(F16)[:, 0:4 * P]).then_inc(xsT_ready[t.par], 1)

                def split_h(t, b):
                    dve.wait_ge(h_hi[t.par], t.par_uses * 2 + (b + 1))
                    dve.tensor_tensor(h_hl[:, t.par, 1, 2 * b:2 * b + 2, :], h_f[:, t.par, 2 * b:2 * b + 2, :],
                                      h_hl[:, t.par, 0, 2 * b:2 * b + 2, :], ALU.subtract).then_inc(h_split[t.par], 1)

                def take_y(t, e):
                    dve.wait_ge(y_done, t.count + 1)
                    if t.ring_reused:
                        dve.wait_ge(y_stored[t.ring], t.ring_uses * DMA)
                    dve.scalar_tensor_tensor(
                        out=y_sb[:, t.ring], in0=y_banks[:, :, 0:D],
                        scalar=1.0 / WS, in1=b2_bc[:, bass.ds(e * D, D)].rearrange("p (o d) -> p o d", o=1)
                        .to_broadcast([P, 2, D]), op0=ALU.mult, op1=ALU.add).then_inc(y_begun, 1)
                    dve.wait_ge(y_begun, t.count + 1)
                    dve.scalar_tensor_tensor(out=y_sb[:, t.ring], in0=y_banks[:, :, D:2 * D], scalar=1.0 / WS,
                                             in1=y_sb[:, t.ring], op0=ALU.mult, op1=ALU.add).then_inc(y_ready, 1)

                def step(t, nxt, prv, old):
                    if not prv:
                        copy_xT(t)
                    if prv:
                        e = dve.value_load(tile_expert[0:1, bass.ds(prv.j, 1)], min_val=0, max_val=E - 1)
                    if nxt:
                        copy_xT(nxt)
                    split_h(t, 0)
                    if prv:
                        take_y(prv, e)
                    split_h(t, 1)
                over_expert_tiles(dve, f, step)
                take_y(last, dve.value_load(tile_expert[0:1, bass.ds(last.j, 1)], min_val=0, max_val=E - 1))

            def first_pass(g, first):
                st = Steps(dve, route_step, g * ROUTE_STEPS)
                dve.wait_ge(x_loaded, (g + 1) * DMA)
                statistics(g * J, 0, st)
                norm(g, g * J, 0, st)
                low_halves(g)
                route(g, g, st, first)
                assert st.n == ROUTE_STEPS, st.n

            first_pass(0, True)
            with dve.Fori(1, G) as g:
                first_pass(g, False)
            split_weights()
            plan(0)
            experts(0)
            next_gather(0)
            st = Steps(dve, out_step, 0)
            combine(0, 0, 0, st)
            next_gather(J * 2)
            dve.wait_ge(combined, C)
            statistics(0, 1, st)
            norm(G, 0, 1, st)
            out_steps_before = st.n

            def second_pass(g, last):
                st = Steps(dve, group_step, g * GROUP_STEPS)
                attention(g, st, last)
                statistics(g * J, 0, st)
                norm(g * 2 + (G + 1), g * J, 0, st)
                if not last:
                    dve.wait_ge(combined, (g + 1) * C + C)
                    statistics((g + 1) * J, 1, st)
                low_halves(g + G)
                if not last:
                    dve.wait_ge(hl_ready, g + (G + 1))
                    dve.wait_ge(xn_turned, (g * 2 + (G + 2)) * C)
                    norm(g * 2 + (G + 2), (g + 1) * J, 1, st)
                route(g + G, g, st)
                assert last or st.n == GROUP_STEPS, st.n

            with dve.Fori(0, G - 1) as g:
                second_pass(g, False)
            second_pass(G - 1, True)
            plan(1)
            experts(1)
            next_gather(0)
            with dve.Fori(0, G) as g:
                st = Steps(dve, out_step, g * (2 * J // 2) + out_steps_before)
                combine(g + G, g * J, g * (J * 2), st)
                next_gather(g * (J * 2) + J * 2)


_INS = ["L0_attn_x", "L0_attn_Wq", "L0_attn_Wk", "L0_attn_Wv", "L0_attn_Wo", "L0_ffn_Wg", "L0_ffn_bg",
        "L0_ffn_W1", "L0_ffn_b1", "L0_ffn_W2", "L0_ffn_b2"]


def kernel(**inputs):
    import numpy as _np
    import concourse.bacc as _bacc
    from concourse import mybir as _mybir
    from concourse.bass_utils import run_bass_kernel_spmd as _run

    nc = _bacc.Bacc("TRN2", target_bir_lowering=False, num_devices=1)
    arrays, args = {}, []
    for name in _INS:
        a = _np.ascontiguousarray(inputs[name])
        arrays[f"in_{name}"] = a
        args.append(nc.dram_tensor(f"in_{name}", a.shape, _mybir.dt.from_np(a.dtype), kind="ExternalInput").ap())
    args.append(nc.dram_tensor("out_0", arrays["in_L0_attn_x"].shape, F32, kind="ExternalOutput").ap())
    macaron(nc, *args)
    r = _run(nc, [arrays], core_ids=[0])
    return r.results[0]["out_0"]
```

```python
from contextlib import ExitStack

import concourse.bass as bass
from concourse import mybir

F32 = mybir.dt.float32
F16 = mybir.dt.float16
BF16 = mybir.dt.bfloat16
I32 = mybir.dt.int32
U32 = mybir.dt.uint32
ALU = mybir.AluOpType
ACT = mybir.ActivationFunctionType
X = mybir.AxisListType.X

P = 128
D = 128
E = 8
H = 512
HC = H // P
HEADS = 16
DK = D // HEADS
RADIUS = 8
W = RADIUS + 1
SCORE_SCALE = 1.0 / (2.0 * 0.28)
LN_EPS = 1e-5
WS = 64.0
LOW = -1e30
J = 16
C = 4
JC = J // C
SLOT_TILE = 256
NJ = 4
SPARE = 12
EU = 16
PEEL = 6
Y_LAG = 6
TOK_RING = 8
ROUTE_STEPS = 56
GROUP_STEPS = 120
PLAN_STEPS = 33
VALUES_HALF = (1, 1, 0, 1)
SCATTER_TILES = (5, 11)
COMBINE_TILES = (3, 6, 9, 12)
DMA = 16


class Steps:

    def __init__(self, eng, sem, before):
        self.eng, self.sem, self.before, self.n = eng, sem, before, 0

    def did(self, ins):
        ins.then_inc(self.sem, 1)
        self.n += 1

    def settle(self):
        if self.n:
            self.eng.wait_ge(self.sem, self.before + self.n)


class Tile:

    def __init__(self, i, first, f, n_tiles):
        def uses(n):
            return i * (EU // n) + (first // n + f * len(range(first % n, n_tiles, n)))
        self.j = i * EU + first
        self.half = 0 if first < n_tiles // 2 else 1
        self.j_in_half = i * EU + (first - self.half * (n_tiles // 2))
        self.ring, self.ring_uses = first % 4, uses(4)
        self.par, self.par_uses = first % 2, uses(2)
        self.tok, self.tok_uses = first % TOK_RING, uses(TOK_RING)
        self.first_of_body = not isinstance(i, int) and first in (PEEL, n_tiles // 2 + PEEL) or \
            isinstance(i, int) and first in (PEEL + 2 * EU, n_tiles - 1)
        self.count = i * EU + (first + f * n_tiles)
        self.not_first = f > 0 or first > 0
        self.ring_reused = f > 0 or first >= 4
        self.par_reused = f > 0 or first >= 2


def macaron(nc, x, Wq, Wk, Wv, Wo, Wg, bg, W1, b1, W2, b2, out):
    B, S, _ = x.shape
    N = B * S
    G = N // (P * J)
    TILES = G * J
    HG = G // 2
    HT = (2 * N // 2 - E) // SLOT_TILE + E
    NT = 2 * HT
    assert HT == PEEL + HG * EU + 1
    SLOTS = E * N + SPARE * SLOT_TILE
    SP_COLS = SLOTS // P
    LOW_SEQ = S // J

    x_hl = nc.dram_tensor("x_hl", [N, 2 * D], F16, kind="Internal").ap()
    slot_token = [[nc.dram_tensor(f"slot_token{h}_{r}", [SLOTS], U32, kind="Internal").ap() for r in range(NJ)]
                  for h in range(2)]
    slot_token_sum = [nc.dram_tensor(f"slot_token_sum{h}", [SLOTS], U32, kind="Internal").ap() for h in range(2)]
    y_rows = [nc.dram_tensor(f"y_rows{h}", [HT * SLOT_TILE, D], F32, kind="Internal").ap() for h in range(2)]

    x_v = x.flatten_outer_dims().rearrange("(g p j) d -> g p (j d)", p=P, j=J)
    out_v = out.flatten_outer_dims().rearrange("(g p j) d -> g p (j d)", p=P, j=J)
    x_hl_v = x_hl.rearrange("(g p j) c -> g p (j c)", p=P, j=J)

    with ExitStack() as ctx:
        def sb(name, shape, dt):
            return ctx.enter_context(nc.sbuf_tensor(name, shape, dt))

        def sem(name):
            return ctx.enter_context(nc.semaphore(name))

        def sems(name, n):
            return [sem(f"{name}{i}") for i in range(n)]

        x_sb = sb("x_sb", [P, TILES * D], F32)
        BLOCKS = 2 * E * HC
        w_hl = sb("w_hl", [P, BLOCKS, 2, P], F16)
        wqkv = sb("wqkv", [P, 3 * D], F32)
        wo_sb = sb("wo_sb", [P, D], F32)
        wg_sb = sb("wg_sb", [P, E], F32)
        bg_bc = sb("bg_bc", [P, E], F32)
        b1_rows = sb("b1_rows", [E * HC, P], F32)
        b1_cols = sb("b1_cols", [P, E * HC], F32)
        b2_bc = sb("b2_bc", [P, E * D], F32)
        ident = sb("ident", [P, P], F32)
        ident16 = sb("ident16", [P, P], F16)
        before16 = sb("before16", [P, P], BF16)
        ones16 = sb("ones16", [P, P], BF16)
        e_iota = sb("e_iota", [P, J * E], F32)
        token_ids = sb("token_ids", [P, TILES], U32)
        window_mask = sb("window_mask", [P, RADIUS * W], F32)
        part_i = sb("part_i", [P, 1], I32)
        seq_start = sb("seq_start", [P, 1], F32)
        gates = sb("gates", [P, TILES * 2], F32)
        slots_all = sb("slots_all", [P, TILES * 2], F32)
        y_row = sb("y_row", [P, (TILES + J) * 2], U32)
        stats = sb("stats", [P, J, 6], F32)
        mean_var = sb("mean_var", [P, J, 2], F32)
        var_eps = sb("var_eps", [P, 2, J], F32)
        std = sb("std", [P, 2, J], F32)
        rstd = sb("rstd", [P, 2, J], F32)
        xn = sb("xn", [P, J, D], F32)
        xnT = sb("xnT", [P, J, D + 2], F32)
        hl = sb("hl", [P, J, 2 * D], F16)
        logits = sb("logits", [P, J * E], F32)
        top = sb("top", [P, 2, J], F32)
        cand = sb("cand", [P, J * E], F32)
        cand2 = sb("cand2", [P, J * E], F32)
        choice = sb("choice", [P, 2, J], F32)
        onehot = sb("onehot", [P, J, 2, E], F32)
        logits2 = sb("logits2", [P, J * E], F32)
        gate_exp = sb("gate_exp", [P, J, E + 1], F32)
        gate_sum = sb("gate_sum", [P, J], F32)
        gate_inv = sb("gate_inv", [P, J], F32)
        chosen = sb("chosen", [P, (J + 1) * E], BF16)
        slot_base = sb("slot_base", [P, 2, E], F32)
        slot_of = sb("slot_of", [P, J * E], F32)
        slot_sel = sb("slot_sel", [P, J, 2, E], F32)
        slot_f = sb("slot_f", [P, J * 2], F32)
        slots_g = sb("slots_g", [P, J * 2], U32)
        ids_g = sb("ids_g", [P, J], U32)
        gather_slots = sb("gather_slots", [P, J * 2], U32)
        y_in = sb("y_in", [P, J, 2, D], F32)
        zeros = y_in[:].rearrange("p j k d -> p (j k d)")[:, 0:SP_COLS].bitcast(U32)
        KV = J + RADIUS
        qkv = sb("qkv", [P, KV, 3 * D], F32)
        prod = sb("prod", [P, 2, JC, W, D], F32)
        score = sb("score", [P, J, W, HEADS], F32)
        smax = sb("smax", [P, J // 2, HEADS], F32)
        ssum = sb("ssum", [P, J * HEADS], F32)
        sinv = sb("sinv", [P, J * HEADS], F32)
        counts_i = sb("counts_i", [P, E], I32)
        n_tiles_i = sb("n_tiles_i", [P, E], I32)
        n_tiles = sb("n_tiles", [P, E], F32)
        earlier = sb("earlier", [P, (E + 1) * E], F32)
        plan_t = sb("plan_t", [P, (E + 1) * E], F32)
        tile_start = sb("tile_start", [P, E + 1], F32)
        region = sb("region", [P, E + 1], F32)
        row_off = sb("row_off", [P, 2, E + 1], F32)
        row_jump = sb("row_jump", [P, 2, E], F32)
        group_end = sb("group_end", [P, G * E], F32)
        half_start = sb("half_start", [P, E + 1], F32)
        tile_no = sb("tile_no", [1, HT], F32)
        tile_expert = sb("tile_expert", [1, NT], I32)
        tile_row = sb("tile_row", [1, NT], I32)
        tile_tok = sb("tile_tok", [P, TOK_RING, 2], U32)
        prod_flat = prod[:].rearrange("p a j w d -> p (a j w d)")
        h_f = prod_flat[:, 0:2 * HC * 256].rearrange("p (a c n) -> p a c n", a=2, c=HC)
        h_hl = prod_flat[:, 2048:2048 + 2048].bitcast(F16).rearrange("p (a s c n) -> p a s c n", a=2, s=2, c=HC)
        xsT = prod_flat[:, 4096:4608].bitcast(F16).rearrange("p (a s i n) -> p a s i n", a=2, s=2, i=2)
        y_sb = prod_flat[:, 4608:5632].rearrange("p (r i d) -> p r i d", r=4, i=2)
        xs = prod_flat[:, 8192:9216].bitcast(F16).rearrange("p (r i c) -> p r i c", r=4, i=2)
        w_stage = prod_flat[:, 0:BLOCKS * P].rearrange("p (n d) -> p n d", d=P)
        class MapsIn:
            def __init__(self, flat):
                self.four = flat[:, 0:NJ * SP_COLS].bitcast(U32).rearrange("p (r n) -> p r n", r=NJ)
                self.sum = flat[:, NJ * SP_COLS:(NJ + 1) * SP_COLS].bitcast(U32)

        qkv_flat = qkv[:].rearrange("p s c -> p (s c)")
        y_in_flat = y_in[:].rearrange("p j k d -> p (j k d)")
        maps_in_qkv, maps_in_y_in = MapsIn(qkv_flat), MapsIn(y_in_flat)

        class PlanScratch:

            def __init__(self, flat):
                e1, row = E + 1, flat[0:1, :]
                self.begun = row[:, 0:(e1 + 1) * HT]
                self.mine = row[:, (e1 + 1) * HT:(2 * e1 + 1) * HT]
                self.mine_w = row[:, (2 * e1 + 1) * HT:(3 * e1 + 1) * HT]
                self.map_f = row[:, (3 * e1 + 1) * HT:(3 * e1 + 3) * HT].rearrange("o (k n) -> o k n", k=2)

        after_maps = (NJ + 1) * SP_COLS
        plan_in_qkv, plan_in_y_in = PlanScratch(qkv_flat[:, after_maps:]), PlanScratch(y_in_flat[:, after_maps:])
        PAIRS = HG * J * 2
        rows_at = [after_maps + k * PAIRS * (E - 1) for k in (0, 1, 2)]
        jumps = [qkv_flat[:, at:at + PAIRS * (E - 1)].rearrange("p (n e) -> p n e", e=E - 1) for at in rows_at[0:2]]
        y_row_f = qkv_flat[:, rows_at[2]:rows_at[2] + PAIRS]
        o_sb = xn
        oT = xnT[:, :, 1:1 + P]

        banks_0_1 = ctx.enter_context(nc.psum_tensor("banks_0_1", [P, 2, 512], F32))
        bank = [banks_0_1[:, 0, :], banks_0_1[:, 1, :]]
        bank += [ctx.enter_context(nc.psum_tensor(f"bank{i}", [P, 512], F32)) for i in range(2, 6)]
        banks_6_7 = ctx.enter_context(nc.psum_tensor("banks_6_7", [P, 2, 512], F32))
        bank += [banks_6_7[:, 0, :], banks_6_7[:, 1, :]]
        y_banks = banks_6_7[:]
        score_banks = banks_0_1[:, :, 0:JC // 2 * W * HEADS]

        consts_loaded = sem("consts_loaded")
        w_loaded = sem("w_loaded")
        w_rounded = sem("w_rounded")
        w_split = sem("w_split")
        x_loaded = sem("x_loaded")
        pool_step = sem("pool_step")
        b1_turned = sem("b1_turned")
        consts_done = sem("consts_done")
        var_ready = sem("var_ready")
        std_ready = sem("std_ready")
        xn_ready = sem("xn_ready")
        xn_turned = sem("xn_turned")
        xnT_ready = sem("xnT_ready")
        logits_ready = sem("logits_ready")
        gate_diff = sem("gate_diff")
        gate_exped = sem("gate_exped")
        chosen_ready = sem("chosen_ready")
        rank_ready = sem("rank_ready")
        hi_ready = sem("hi_ready")
        hl_ready = sem("hl_ready")
        hl_stored = sem("hl_stored")
        slots_ready = sem("slots_ready")
        map_cleared = sems("map_cleared", NJ)
        map_scattered = sems("map_scattered", NJ)
        maps_loaded = sem("maps_loaded")
        maps_partly = sem("maps_partly")
        maps_added = sem("maps_added")
        map_stored = sem("map_stored")
        plan_ready = sem("plan_ready")
        gather_slots_ready = sem("gather_slots_ready")
        y_gathered = sems("y_gathered", C)
        combined = sem("combined")
        qkv_done = sem("qkv_done")
        qkv_ready = sem("qkv_ready")
        keys_multiplied = sem("keys_multiplied")
        channels_added = sem("channels_added")
        score_ready = sem("score_ready")
        prob_ready = sem("prob_ready")
        pv_ready = sem("pv_ready")
        pv_summed = sem("pv_summed")
        o_ready = sem("o_ready")
        o_turned = sem("o_turned")
        oT_ready = sem("oT_ready")
        attn_done = sem("attn_done")
        attn_added = sem("attn_added")
        out_stored = sem("out_stored")
        tok_loaded = sems("tok_loaded", TOK_RING)
        xs_gathered = sems("xs_gathered", 4)
        xs_turned = sems("xs_turned", 4)
        xsT_ready = sems("xsT_ready", 2)
        h_done = sems("h_done", 2)
        h_gelu = sems("h_gelu", 2)
        h_hi = sems("h_hi", 2)
        h_split = sems("h_split", 2)
        y_done = sem("y_done")
        y_begun = sem("y_begun")
        y_ready = sem("y_ready")
        y_stored = sems("y_stored", 4)
        waits_carried = sem("waits_carried")
        setup_step = sem("setup_step")
        route_step = sem("route_step")
        group_step = sem("group_step")
        plan_step = sem("plan_step")
        out_step = sem("out_step")

        N_CONSTS = 8
        SC = 2 * J // NJ
        SUMS = 1 + HG
        SUM_TILE = 11

        def xt(t, n=1):
            return x_sb[:, bass.ds(t * D, n * D)]

        def over_expert_tiles(eng, f, step, before=None, with_first=None, with_second=None):
            def at(i, first):
                return Tile(i, first, f, NT) if 0 <= first < NT else None

            def one(i, first):
                step(at(i, first), at(i, first + 1), at(i, first - 1), at(i, first - Y_LAG))

            def straight(lo, hi):
                for first in range(lo, hi):
                    if before and first in before:
                        before[first]()
                    one(0, first)

            def turns(lo, also):
                with eng.Fori(0, HG) as i:
                    for k in range(EU):
                        if also and k == 0:
                            also(i, -1)
                        one(i, lo + k)
                        if also:
                            also(i, k)

            straight(0, PEEL)
            turns(PEEL, with_first)
            straight(PEEL + HG * EU, HT + PEEL)
            turns(HT + PEEL, with_second)
            straight(NT - 1, NT)

        def spread(n, k, start, end):
            return [n * min(max(0, m - start), end - start) // (end - start) for m in (k, k + 1)]

        def carry_waits(eng):
            eng.sem_inc(waits_carried)

        block = ctx.enter_context(nc.Block())

        @block.sync
        def _(sp):
            sp.dma_start(x_sb[:, 0:J * D], x_v[0]).then_inc(x_loaded, DMA)
            for dst, src in ((wg_sb[:], Wg), (bg_bc[:], bg.rearrange("(o e) -> o e", o=1).to_broadcast([P, E])),
                             (b1_rows[:], b1.rearrange("e (c p) -> (e c) p", p=P)),
                             (wqkv[:, 0:D], Wq), (wqkv[:, D:2 * D], Wk), (wqkv[:, 2 * D:], Wv), (wo_sb[:], Wo),
                             (b2_bc[:], b2.rearrange("(o e) d -> o (e d)", o=1).to_broadcast([P, E * D]))):
                sp.dma_start(dst, src).then_inc(consts_loaded, DMA)
            for g in range(1, G):
                sp.wait_ge(x_loaded, g * DMA)
                sp.dma_start(x_sb[:, g * J * D:(g + 1) * J * D], x_v[g]).then_inc(x_loaded, DMA)
            def clear_maps(h):
                for r in range(NJ):
                    sp.dma_start(slot_token[h][r].rearrange("(p n) -> p n", p=P), zeros).then_inc(map_cleared[r], DMA)

            sp.wait_ge(pool_step, 1)
            clear_maps(0)
            sp.dma_start(w_stage[:, 0:BLOCKS // 2].rearrange("p (e c) d -> p e (c d)", e=E),
                         W1.rearrange("e d h -> d e h")).then_inc(w_loaded, DMA)
            sp.dma_start(w_stage[:, BLOCKS // 2:].rearrange("p (e c) d -> p e c d", e=E),
                         W2.rearrange("e (c p) d -> p e c d", p=P)).then_inc(w_loaded, DMA)
            clear_maps(1)

            def store_hl(q, g):
                sp.wait_ge(hl_ready, q + 1)
                sp.dma_start(x_hl_v[bass.ds(g, 1)].rearrange("a p n -> (a p) n"),
                             hl[:].rearrange("p j c -> p (j c)")).then_inc(hl_stored, DMA)

            def load_maps(u, half, scatters, maps):
                for r in range(NJ):
                    sp.wait_ge(map_scattered[r], scatters * DMA)
                    sp.dma_start(maps.four[:, r, :], slot_token[half][r].rearrange("(p n) -> p n", p=P)).then_inc(maps_loaded, DMA)

            def store_map(u, half, maps):
                sp.wait_ge(maps_added, u + 1)
                sp.dma_start(slot_token_sum[half].rearrange("(p n) -> p n", p=P), maps.sum).then_inc(map_stored, DMA)

            def store_y(t):
                sp.wait_ge(y_ready, t.count + 1)
                sp.dma_start(y_rows[t.half][bass.ds(t.j_in_half * SLOT_TILE, SLOT_TILE), :].rearrange("(p i) d -> p (i d)", i=2),
                              y_sb[:, t.ring].rearrange("p i d -> p (i d)")).then_inc(y_stored[t.ring], DMA)

            def tile_tokens(f):
                sp.wait_ge(map_stored, (SUMS * f + 1) * DMA)
                sp.wait_ge(plan_ready, 2 * f + 1)

                def second_map(i, k):
                    if k == SUM_TILE:
                        load_maps(i + (SUMS * f + 1), 1, i * (J // NJ) + ((2 * G - 1 + (f - 1) * G) * SC + J // NJ), maps_in_qkv)
                    elif k == EU - 1:
                        store_map(i + (SUMS * f + 1), 1, maps_in_qkv)

                def second_half():
                    sp.wait_ge(map_stored, SUMS * (f + 1) * DMA)
                    sp.wait_ge(plan_ready, 2 * f + 2)

                def load_tokens(t):
                    row = sp.value_load(tile_row[0:1, bass.ds(t.j, 1)], min_val=0, max_val=SLOTS - SLOT_TILE)
                    sp.dma_start(tile_tok[:, t.tok, :], slot_token_sum[t.half][bass.ds(row, SLOT_TILE)]
                                 .rearrange("(p i) -> p i", i=2)).then_inc(tok_loaded[t.tok], DMA)

                def step(t, nxt, prv, old):
                    if nxt:
                        load_tokens(nxt)
                    if old:
                        store_y(old)
                load_tokens(Tile(0, 0, f, NT))
                before = {HT - 1: second_half}
                if f == 0:
                    before[HT + 2] = lambda: clear_maps(1)
                over_expert_tiles(sp, f, step, before, second_map)
                for k in range(NT - Y_LAG, NT):
                    store_y(Tile(0, k, f, NT))

            with sp.Fori(0, G) as g:
                store_hl(g, g)
            load_maps(0, 0, HG * SC, maps_in_qkv)
            store_map(0, 0, maps_in_qkv)
            clear_maps(0)
            tile_tokens(0)
            with sp.Fori(0, G - 1) as g:
                store_hl(g + G, g)
            sp.wait_ge(combined, G * C)
            load_maps(SUMS, 0, (G + HG) * SC, maps_in_y_in)
            store_map(SUMS, 0, maps_in_y_in)
            store_hl(2 * G - 1, G - 1)
            tile_tokens(1)
            with sp.Fori(0, G) as g:
                sp.wait_ge(combined, (g + G + 1) * C)
                sp.dma_start(out_v[bass.ds(g, 1)].rearrange("a p n -> (a p) n"),
                             xt(g * J, J)).then_inc(out_stored, DMA)
            sp.wait_ge(out_stored, G * DMA)

        @block.gpsimd
        def _(pool):
            pool.memset(zeros, 0).then_inc(pool_step, 1)
            pool.memset(ident[:], 0.0).then_inc(pool_step, 1)
            pool.memset(ident16[:], 0.0).then_inc(pool_step, 1)
            pool.memset(before16[:], 1.0).then_inc(pool_step, 1)
            pool.memset(window_mask[:], 0.0).then_inc(pool_step, 1)
            pool.memset(earlier[:], 1.0).then_inc(pool_step, 1)
            pool.wait_ge(pool_step, 6)
            pool.affine_select(out=ident[:], in_=ident[:], compare_op=ALU.not_equal, fill=1.0, base=0,
                               pattern=[[-1, P]], channel_multiplier=1).then_inc(pool_step, 1)
            pool.affine_select(out=ident16[:], in_=ident16[:], compare_op=ALU.not_equal, fill=1.0, base=0,
                               pattern=[[-1, P]], channel_multiplier=1).then_inc(pool_step, 1)
            pool.affine_select(out=before16[:], in_=before16[:], compare_op=ALU.is_gt, fill=0.0, base=0,
                               pattern=[[1, P]], channel_multiplier=-1).then_inc(pool_step, 1)
            pool.affine_select(out=window_mask[:].rearrange("p (j w) -> p j w", w=W),
                               in_=window_mask[:].rearrange("p (j w) -> p j w", w=W), compare_op=ALU.is_ge,
                               fill=LOW, base=-RADIUS, pattern=[[1, RADIUS], [1, W]],
                               channel_multiplier=0).then_inc(pool_step, 1)
            pool.affine_select(out=earlier[:].rearrange("o (e f) -> o e f", f=E),
                               in_=earlier[:].rearrange("o (e f) -> o e f", f=E), compare_op=ALU.is_gt,
                               fill=0.0, base=0, pattern=[[1, E + 1], [-1, E]],
                               channel_multiplier=0).then_inc(pool_step, 1)
            pool.iota(e_iota[:].rearrange("p (j e) -> p j e", e=E), [[0, J], [1, E]], base=0,
                      channel_multiplier=0, allow_small_or_imprecise_dtypes=True).then_inc(pool_step, 1)
            pool.iota(token_ids[:].rearrange("p (g j) -> p g j", j=J), [[P * J, G], [1, J]], base=0,
                      channel_multiplier=J).then_inc(pool_step, 1)
            pool.iota(part_i[:], [[0, 1]], base=0, channel_multiplier=1).then_inc(pool_step, 1)
            pool.iota(slot_base[:], [[0, 2], [N, E]], base=0, channel_multiplier=0,
                      allow_small_or_imprecise_dtypes=True).then_inc(pool_step, 1)
            pool.iota(region[:], [[N, E + 1]], base=0, channel_multiplier=0,
                      allow_small_or_imprecise_dtypes=True).then_inc(pool_step, 1)
            pool.iota(tile_no[:], [[1, HT]], base=0, channel_multiplier=0,
                      allow_small_or_imprecise_dtypes=True).then_inc(pool_step, 1)
            pool.memset(ones16[:], 1.0).then_inc(pool_step, 1)
            pool.memset(chosen[:], 0.0).then_inc(pool_step, 1)
            pool.memset(xnT[:], 0.0).then_inc(pool_step, 1)
            pool.memset(y_row[:], 0).then_inc(pool_step, 1)
            pool.wait_ge(pool_step, 21)

            def scatter_ids(q, half, clears, base=None, part=(0, J * 2)):
                base = q * SC if base is None else base
                if part[0] == 0 < part[1]:
                    pool.wait_ge(slots_ready, q + 1)
                for i in range(*part):
                    r, m = i % NJ, i // NJ
                    if m > 0 or not (isinstance(q, int) and q == 0):
                        pool.wait_ge(map_scattered[r], (base + m) * DMA)
                    pool.wait_ge(map_cleared[r], clears * DMA)
                    carry_waits(pool)
                    pool.indirect_dma_start(
                        out=slot_token[half][r].rearrange("(n o) -> n o", o=1),
                        out_offset=bass.IndirectOffsetOnAxis(ap=slots_g[:, i:i + 1], axis=0),
                        in_=ids_g[:, i // 2:i // 2 + 1], in_offset=None).then_inc(map_scattered[r], DMA)

            def gather_y(cr, half, first, cf, part=(0, J * 2)):
                if part[0] == 0:
                    pool.wait_ge(gather_slots_ready, cr + (1 + cf))
                for i in range(*part):
                    c, in_chunk = i // (JC * 2), i % (JC * 2)
                    if in_chunk == 0:
                        if not first:
                            pool.wait_ge(combined, cr * C + (c + 1 - C))
                        carry_waits(pool)
                    pool.indirect_dma_start(
                        out=y_in[:, i // 2, i % 2, :], out_offset=None, in_=y_rows[half],
                        in_offset=bass.IndirectOffsetOnAxis(ap=gather_slots[:, i:i + 1], axis=0)
                    ).then_inc(y_gathered[c], DMA)

            def gather_tokens(f):
                pool.wait_ge(hl_stored, (f + 1) * G * DMA)

                def step(t, nxt, prv, old):
                    pool.wait_ge(tok_loaded[t.tok], (t.tok_uses + 1) * DMA)
                    if t.ring_reused:
                        pool.wait_ge(xs_turned[t.ring], t.ring_uses)
                    carry_waits(pool)
                    for half in range(2):
                        pool.indirect_dma_start(
                            out=xs[:, t.ring, half, :], out_offset=None, in_=x_hl,
                            in_offset=bass.IndirectOffsetOnAxis(ap=tile_tok[:, t.tok, half:half + 1], axis=0)
                        ).then_inc(xs_gathered[t.ring], DMA)

                def scatter_along(i, k):
                    if k < 0:
                        return
                    scatter_ids(i + ((G + 1) * f + G - 1), 1, 2 * (f + 1), base=i * (J // NJ) + (G * f + G - 1) * SC,
                                part=spread(J, k, *SCATTER_TILES))

                def gather_along(i, k):
                    if k == -1:
                        for s in range(4):
                            pool.wait_ge(y_stored[s], DMA * (len(range(s, HT, 4)) + f * len(range(s, NT, 4))))
                    elif k < COMBINE_TILES[-1]:
                        c = sum(k >= tile for tile in COMBINE_TILES)
                        n = spread(2 * JC, k, COMBINE_TILES[c - 1] if c else 0, COMBINE_TILES[c])
                        gather_y(i + G, 0, False, 1, part=[c * (2 * JC) + m for m in n])
                over_expert_tiles(pool, f, step, None, scatter_along, gather_along if f == 1 else None)
                for s in range(4):
                    pool.wait_ge(y_stored[s], DMA * (f + 1) * len(range(s, NT, 4)))

            for g in range(HG):
                scatter_ids(g, 0, 2)
            scatter_ids(HG, 1, 2)
            gather_tokens(0)
            for r in range(NJ):
                pool.wait_ge(map_cleared[r], 4 * DMA)
            gather_y(0, 0, True, 0)
            gather_y(1, 0, False, 0)
            with pool.Fori(0, HG) as g:
                gather_y(g + HG, 1, False, 0)
                scatter_ids(g + (G + 1), 0, 4, base=(g + G) * SC)
            scatter_ids(2 * G - 1, 1, 4, base=(2 * G - 2) * SC)
            gather_tokens(1)
            with pool.Fori(HG, G) as g:
                gather_y(g + G, 1, False, 1)

        @block.scalar
        def _(act):
            act.wait_ge(b1_turned, 1)
            act.copy(b1_cols[:], bank[0][:, 0:E * HC]).then_inc(consts_done, 1)

            def sqrt(v, kind):
                act.wait_ge(var_ready, v + 1)
                act.activation(std[:, kind, :], var_eps[:, kind, :], ACT.Sqrt).then_inc(std_ready, 1)

            def copy_xnT(r):
                for c in range(C):
                    act.wait_ge(xn_turned, r * C + (c + 1))
                    act.copy(xnT[:, c * JC:(c + 1) * JC, 1:1 + P],
                             bank[c % 2][:].rearrange("p (j n) -> p j n", n=P)).then_inc(xnT_ready, 1)

            def copy_hi(r):
                act.wait_ge(xn_ready, r * C + C)
                act.copy(hl[:, :, 0:D], xn[:]).then_inc(hi_ready, 1)

            def gate_exponentials(q):
                act.wait_ge(gate_diff, q + 1)
                act.activation(gate_exp[:], gate_exp[:], ACT.Exp).then_inc(gate_exped, 1)

            def copy_qkv(g, between=None):
                for k in range(KV):
                    if k == RADIUS and between:
                        between()
                    act.wait_ge(qkv_done, g * KV + (k + 1))
                    lo = D if k < RADIUS else 0
                    act.copy(qkv[:, k, lo:3 * D], bank[4 + k % 2][:, lo:3 * D]).then_inc(qkv_ready, 1)

            def attention(g):
                for h in range(2):
                    mine = score[:, h * J // 2:(h + 1) * J // 2]
                    act.wait_ge(score_ready, g * 2 + (h + 1))
                    act.activation(mine, mine, ACT.Exp, scale=SCORE_SCALE).then_inc(prob_ready, 1)
                for c in range(C):
                    act.wait_ge(o_turned, g * C + (c + 1))
                    act.copy(oT[:, c * JC:(c + 1) * JC, :],
                             bank[c % 2][:].rearrange("p (j n) -> p j n", n=P)).then_inc(oT_ready, 1)

            def experts(f):
                act.wait_ge(plan_ready, 2 * f + 1)

                def step(t, nxt, prv, old):
                    e = act.value_load(tile_expert[0:1, bass.ds(t.j, 1)], min_val=0, max_val=E - 1)
                    for b in range(2):
                        act.wait_ge(h_done[t.par], t.par_uses * 2 + (b + 1))
                        if t.par_reused:
                            act.wait_ge(h_split[t.par], t.par_uses * 2)
                        for c in (2 * b, 2 * b + 1):
                            ins = act.activation(h_f[:, t.par, c, :], bank[2 + 2 * t.par + b][:, (c % 2) * 256:(c % 2 + 1) * 256],
                                                 ACT.Gelu, bias=b1_cols[:, bass.ds(e * HC + c, 1)], scale=1.0 / WS)
                        ins.then_inc(h_gelu[t.par], 1)
                        act.wait_ge(h_gelu[t.par], t.par_uses * 2 + (b + 1))
                        if t.par_reused:
                            act.wait_ge(y_done, t.count - 1)
                        act.copy(h_hl[:, t.par, 0, 2 * b:2 * b + 2, :],
                                 h_f[:, t.par, 2 * b:2 * b + 2, :]).then_inc(h_hi[t.par], 1)
                over_expert_tiles(act, f, step, {HT: lambda: act.wait_ge(plan_ready, 2 * f + 2)})

            def first_pass(g):
                sqrt(g, 0)
                copy_xnT(g)
                copy_hi(g)
                gate_exponentials(g)
                act.wait_ge(hl_stored, (g + 1) * DMA)

            def round_weights(part):
                n = BLOCKS // 2
                act.activation(w_hl[:, part * n:(part + 1) * n, 0, :], w_stage[:, part * n:(part + 1) * n, :],
                               ACT.Copy, scale=WS).then_inc(w_rounded, 1)

            first_pass(0)
            first_pass(1)
            act.wait_ge(w_loaded, 2 * DMA)
            round_weights(0)
            round_weights(1)
            with act.Fori(2, G) as g:
                first_pass(g)
            experts(0)

            def second_pass(g, last):
                attention(g)
                sqrt(g * 2 + (G + 1), 0)
                copy_xnT(g * 2 + (G + 1))
                act.wait_ge(hl_stored, (g + G) * DMA)
                copy_hi(g * 2 + (G + 1))
                if last:
                    gate_exponentials(g + G)
                else:
                    sqrt(g * 2 + (G + 2), 1)
                    act.wait_ge(logits_ready, g + (G + 1))
                    copy_xnT(g * 2 + (G + 2))
                    copy_qkv(g + 1, lambda: gate_exponentials(g + G))

            sqrt(G, 1)
            copy_xnT(G)
            copy_qkv(0)
            with act.Fori(0, G - 1) as g:
                second_pass(g, False)
            second_pass(G - 1, True)
            experts(1)

        @block.tensor
        def _(pe):
            pe.wait_ge(consts_loaded, N_CONSTS * DMA)
            pe.wait_ge(pool_step, 21)
            pe.transpose(bank[0][:, 0:E * HC], b1_rows[:], ident[0:E * HC, 0:E * HC]).then_inc(b1_turned, 1)
            pe.wait_ge(consts_done, 1)

            def norm(r, route_logits=False):
                for c in range(C + 1):
                    if c < C:
                        pe.wait_ge(xn_ready, r * C + (c + 1))
                        if c >= 2:
                            pe.wait_ge(xnT_ready, r * C + (c - 1))
                        for j in range(JC):
                            ins = pe.transpose(bank[c % 2][:, j * P:(j + 1) * P], xn[:, c * JC + j, :], ident[:])
                        ins.then_inc(xn_turned, 1)
                    if c > 0 and route_logits:
                        pe.wait_ge(xnT_ready, r * C + c)
                        for j in range((c - 1) * JC, c * JC):
                            ins = pe.matmul(bank[2][:, j * E:(j + 1) * E], xnT[:, j, 1:1 + P], wg_sb[:],
                                            start=True, stop=True)
                if route_logits:
                    ins.then_inc(logits_ready, 1)

            def rank(q):
                pe.wait_ge(chosen_ready, q + 1)
                pe.matmul(bank[3][:, 0:(J + 1) * E], before16[:], chosen[:], start=True, stop=False)
                for j in range(J):
                    ins = pe.matmul(bank[3][:, (j + 1) * E:(J + 1) * E].rearrange("p (n e) -> p n e", e=E), ones16[:],
                                    chosen[:, j * E:(j + 1) * E].rearrange("p (o e) -> p o e", o=1)
                                    .to_broadcast([P, J - j, E]), start=False, stop=(j == J - 1))
                ins.then_inc(rank_ready, 1)

            def make_qkv(g, r, between=None):
                pe.wait_ge(xnT_ready, r * C + C)
                for k in range(KV):
                    if k == RADIUS and between:
                        between()
                    if k >= 2:
                        pe.wait_ge(qkv_ready, g * KV + (k - 1))
                    if k < RADIUS:
                        pe.matmul(bank[4 + k % 2][:, D:3 * D], xnT[:, J - RADIUS + k, 0:P], wqkv[:, D:3 * D],
                                  start=True, stop=True).then_inc(qkv_done, 1)
                    else:
                        pe.matmul(bank[4 + k % 2][:, 0:3 * D], xnT[:, k - RADIUS, 1:1 + P], wqkv[:],
                                  start=True, stop=True).then_inc(qkv_done, 1)

            def attention(g):
                pe.wait_ge(keys_multiplied, g + 1)
                products = prod[:, 1].rearrange("p (a j) w (h d) -> p a (j w h) d", a=2, d=DK)
                for half in range(2):
                    for d in range(DK):
                        ins = pe.matmul(score_banks[:, half, :], ident[:], products[:, half, :, d],
                                        start=(d == 0), stop=(d == DK - 1))
                ins.then_inc(channels_added, 1)

                def add_window(c):
                    pe.wait_ge(pv_ready, g * C + (c + 1))
                    if c >= 2:
                        pe.wait_ge(o_ready, g * C + (c - 1))
                    for w in range(W):
                        ins = pe.matmul(bank[6 + c % 2][:].rearrange("p (j d) -> p j d", d=D), ident[:],
                                        prod[:, VALUES_HALF[c], :, w, :], start=(w == 0), stop=(w == W - 1))
                    ins.then_inc(pv_summed, 1)

                def turn_o(c):
                    pe.wait_ge(o_ready, g * C + (c + 1))
                    if c >= 2:
                        pe.wait_ge(oT_ready, g * C + (c - 1))
                    for j in range(JC):
                        ins = pe.transpose(bank[c % 2][:, j * P:(j + 1) * P], o_sb[:, c * JC + j, :], ident[:])
                    ins.then_inc(o_turned, 1)

                def project(c):
                    pe.wait_ge(oT_ready, g * C + (c + 1))
                    if c >= 2:
                        pe.wait_ge(attn_added, g * C + (c - 1))
                    for j in range(JC):
                        ins = pe.matmul(bank[4 + c % 2][:, j * D:(j + 1) * D], oT[:, c * JC + j, :], wo_sb[:],
                                        start=True, stop=True)
                    ins.then_inc(attn_done, 1)

                for c in range(C + 2):
                    if c < C:
                        add_window(c)
                    if 1 <= c <= C:
                        turn_o(c - 1)
                    if c >= 2:
                        project(c - 2)

            def experts(f):
                pe.wait_ge(plan_ready, 2 * f + 1)
                pe.wait_ge(w_split, 2)

                def turn(t):
                    pe.wait_ge(xs_gathered[t.ring], (t.ring_uses + 1) * 2 * DMA)
                    if t.par_reused:
                        pe.wait_ge(xsT_ready[t.par], t.par_uses)
                    for s in range(2):
                        for half in range(2):
                            at = (2 * s + half) * P
                            ins = pe.transpose(bank[t.par][:].bitcast(F16)[:, at:at + P],
                                               xs[:, t.ring, half, s * D:(s + 1) * D], ident16[:])
                    ins.then_inc(xs_turned[t.ring], 1)

                def expert_of(t):
                    return pe.value_load(tile_expert[0:1, bass.ds(t.j, 1)], min_val=0, max_val=E - 1)

                w_flat = w_hl[:].rearrange("p n s d -> p (n s d)")

                def up(t, e):
                    pe.wait_ge(xsT_ready[t.par], t.par_uses + 1)
                    if t.par_reused:
                        pe.wait_ge(h_gelu[t.par], t.par_uses * 2)
                    for c in range(HC):
                        dst = bank[2 + 2 * t.par + c // 2][:, (c % 2) * 256:(c % 2 + 1) * 256]
                        for n, (ws, s) in enumerate(((0, 0), (0, 1), (1, 0))):
                            ins = pe.matmul(dst, w_flat[:, bass.ds((e * HC + c) * (2 * P) + ws * P, P)],
                                            xsT[:, t.par, s].rearrange("p i n -> p (i n)"), start=(n == 0), stop=(n == 2))
                        if c % 2:
                            ins.then_inc(h_done[t.par], 1)

                def down(t, e):
                    if t.not_first:
                        pe.wait_ge(y_ready, t.count)
                    for c in range(HC):
                        if c % 2 == 0:
                            pe.wait_ge(h_split[t.par], t.par_uses * 2 + (c // 2 + 1))
                        at = (e * HC + (c + E * HC)) * (2 * D)
                        for half in range(2):
                            pe.matmul(y_banks[:, half, 0:2 * D], h_hl[:, t.par, 0, c, half * P:(half + 1) * P],
                                      w_flat[:, bass.ds(at, 2 * D)], start=(c == 0), stop=False)
                            ins = pe.matmul(y_banks[:, half, 0:D], h_hl[:, t.par, 1, c, half * P:(half + 1) * P],
                                            w_flat[:, bass.ds(at, D)], start=False, stop=(c == HC - 1))
                    ins.then_inc(y_done, 1)

                e_prv = None

                def step(t, nxt, prv, old):
                    nonlocal e_prv
                    if not prv:
                        turn(t)
                    if prv and t.first_of_body:
                        e_prv = expert_of(prv)
                    e = expert_of(t)
                    up(t, e)
                    if nxt:
                        turn(nxt)
                    if prv:
                        down(prv, e_prv)
                    e_prv = e
                over_expert_tiles(pe, f, step, {HT: lambda: pe.wait_ge(plan_ready, 2 * f + 2)})
                down(Tile(0, NT - 1, f, NT), e_prv)

            with pe.Fori(0, G) as g:
                norm(g, route_logits=True)
                rank(g)
            experts(0)
            norm(G)
            make_qkv(0, G)
            with pe.Fori(0, G - 1) as g:
                attention(g)
                norm(g * 2 + (G + 1), route_logits=True)
                norm(g * 2 + (G + 2))
                make_qkv(g + 1, g * 2 + (G + 2), lambda: rank(g + G))
            attention(G - 1)
            norm(3 * G - 1, route_logits=True)
            rank(2 * G - 1)
            experts(1)

        @block.vector
        def _(dve):
            dve.wait_ge(pool_step, 21)
            su = Steps(dve, setup_step, 0)
            su.did(dve.tensor_scalar(part_i[:], part_i[:], LOW_SEQ - 1, None, ALU.bitwise_and))
            su.settle()
            su.did(dve.tensor_scalar(seq_start[:], part_i[:], 0.0, None, ALU.is_equal))
            su.settle()
            su.did(dve.tensor_scalar(window_mask[:], window_mask[:], seq_start[:], None, ALU.mult))
            su.settle()
            dve.wait_ge(consts_loaded, N_CONSTS * DMA)

            def chunk_statistics(t0, c, st):
                carry_waits(dve)
                for j in range(c * JC, (c + 1) * JC):
                    st.did(dve.bn_stats(stats[:, j, :], xt(t0 + j)))

            def statistics(t0, kind, st, chunks_done=False):
                if not chunks_done:
                    for c in range(C):
                        chunk_statistics(t0, c, st)
                st.settle()
                carry_waits(dve)
                for j in range(J):
                    st.did(dve.bn_aggr(mean_var[:, j, :], stats[:, j, :]))
                st.settle()
                dve.tensor_scalar(var_eps[:, kind, :], mean_var[:, :, 1], LN_EPS, None, ALU.add).then_inc(var_ready, 1)

            def norm(r, t0, kind, st):
                dve.wait_ge(std_ready, r + 1)
                st.did(dve.reciprocal(rstd[:, kind, :], std[:, kind, :]))
                st.settle()
                for c in range(C):
                    for j in range(c * JC, (c + 1) * JC):
                        ins = dve.tensor_scalar(xn[:, j, :], xt(t0 + j), mean_var[:, j, 0:1], rstd[:, kind, j:j + 1],
                                                ALU.subtract, ALU.mult)
                    ins.then_inc(xn_ready, 1)

            def per_e(ap):
                return ap.rearrange("p (j e) -> p j e", e=E)

            def bc_e(ap):
                return ap.rearrange("p (j o) -> p j o", o=1).to_broadcast([P, J, E])

            def offer_slots(first, scatters, at_slot, n):
                if not first:
                    for r in range(NJ):
                        dve.wait_ge(map_scattered[r], scatters * DMA)
                carry_waits(dve)
                dve.tensor_copy(ids_g[:, 0:n // 2], token_ids[:, bass.ds(at_slot // 2, n // 2)])
                dve.tensor_copy(slots_g[:, 0:n], slots_all[:, bass.ds(at_slot, n)]).then_inc(slots_ready, 1)

            def low_halves(q):
                dve.wait_ge(hi_ready, q + 1)
                dve.tensor_tensor(hl[:, :, D:2 * D], xn[:], hl[:, :, 0:D], ALU.subtract).then_inc(hl_ready, 1)

            def route(q, g, st):
                dve.wait_ge(logits_ready, q + 1)
                st.did(dve.tensor_tensor(per_e(logits[:]), per_e(bank[2][:, 0:J * E]),
                                         bg_bc[:].rearrange("p (o e) -> p o e", o=1).to_broadcast([P, J, E]), ALU.add))
                st.settle()
                for k, source in ((0, logits), (1, logits2)):
                    st.did(dve.tensor_reduce(top[:, k, :], per_e(source[:]), X, ALU.max))
                    st.settle()
                    st.did(dve.tensor_tensor(per_e(cand[:]), per_e(source[:]), bc_e(top[:, k, :]), ALU.not_equal))
                    st.settle()
                    st.did(dve.scalar_tensor_tensor(out=cand2[:], in0=cand[:], scalar=float(E), in1=e_iota[:],
                                                    op0=ALU.mult, op1=ALU.add))
                    st.settle()
                    st.did(dve.tensor_reduce(choice[:, k, :], per_e(cand2[:]), X, ALU.min))
                    st.settle()
                    st.did(dve.tensor_tensor(onehot[:, :, k, :], per_e(e_iota[:]), bc_e(choice[:, k, :]), ALU.is_equal))
                    st.settle()
                    if k == 0:
                        st.did(dve.scalar_tensor_tensor(out=per_e(logits2[:]), in0=onehot[:, :, 0, :], scalar=LOW,
                                                        in1=per_e(logits[:]), op0=ALU.mult, op1=ALU.add))
                        st.settle()
                dve.tensor_tensor(per_e(chosen[:, 0:J * E]), onehot[:, :, 0, :], onehot[:, :, 1, :],
                                  ALU.add).then_inc(chosen_ready, 1)
                st.did(dve.tensor_tensor(gate_exp[:, :, 0:E], per_e(logits[:]), bc_e(top[:, 0, :]), ALU.subtract))
                dve.tensor_tensor(gate_exp[:, :, E], top[:, 1, :], top[:, 0, :], ALU.subtract).then_inc(gate_diff, 1)
                dve.wait_ge(rank_ready, q + 1)
                st.did(dve.tensor_tensor(per_e(slot_of[:]), per_e(bank[3][:, 0:J * E]),
                                         slot_base[:, 0, :].rearrange("p (o e) -> p o e", o=1).to_broadcast([P, J, E]),
                                         ALU.add))
                st.settle()
                st.did(dve.tensor_tensor(slot_base[:, 0, :], bank[3][:, J * E:(J + 1) * E], slot_base[:, 0, :], ALU.add))
                st.did(dve.tensor_tensor(slot_sel[:], onehot[:],
                                         slot_of[:].rearrange("p (j o e) -> p j o e", o=1, e=E)
                                         .to_broadcast([P, J, 2, E]), ALU.mult))
                st.settle()
                st.did(dve.tensor_reduce(slot_f[:], slot_sel[:].rearrange("p j k e -> p (j k) e"), X, ALU.add))
                st.settle()
                st.did(dve.tensor_copy(slots_all[:, bass.ds(g * (J * 2), J * 2)], slot_f[:]))
                st.settle()
                st.did(dve.tensor_copy(group_end[:, bass.ds(g * E, E)], slot_base[:, 0, :]))
                dve.wait_ge(gate_exped, q + 1)
                st.did(dve.tensor_reduce(gate_sum[:], gate_exp[:, :, 0:E], X, ALU.add))
                st.settle()
                st.did(dve.reciprocal(gate_inv[:], gate_sum[:]))
                st.settle()
                mine2 = gates[:, bass.ds(g * (J * 2), J * 2)].rearrange("p (j k) -> p j k", k=2)
                st.did(dve.tensor_scalar(mine2[:, :, 0], gate_inv[:], 0.5, None, ALU.mult))
                st.did(dve.scalar_tensor_tensor(out=mine2[:, :, 1], in0=gate_exp[:, :, E], scalar=0.5,
                                                in1=gate_inv[:], op0=ALU.mult, op1=ALU.mult))

            def combine(cr, t0, g2, st, chunks=range(C)):
                for c in chunks:
                    dve.wait_ge(y_gathered[c], (cr + 1) * (2 * JC * DMA))
                    for k in range(2):
                        for j in range(c * JC, (c + 1) * JC):
                            ins = dve.scalar_tensor_tensor(out=xt(t0 + j), in0=y_in[:, j, k, :],
                                                           scalar=gates[:, bass.ds(g2 + (2 * j + k), 1)],
                                                           in1=xt(t0 + j), op0=ALU.mult, op1=ALU.add)
                            if k == 0:
                                st.did(ins)
                        if k == 0:
                            st.settle()
                    ins.then_inc(combined, 1)

            def next_gather(g2):
                dve.tensor_copy(gather_slots[:], y_row[:, bass.ds(g2, J * 2)]).then_inc(gather_slots_ready, 1)

            def attention(g, st, last):
                HJ = J // 2
                keys_half = (0, 1, 0, 0)

                def multiply_keys(c):
                    lo = c * JC
                    dve.wait_ge(qkv_ready, g * KV + (RADIUS + (c + 1) * JC))
                    st.settle()
                    q_ap = qkv[:, RADIUS + lo:RADIUS + lo + JC, 0:D].rearrange("p j (o d) -> p j o d", o=1)
                    ins = dve.tensor_tensor(prod[:, keys_half[c]], q_ap.to_broadcast([P, JC, W, D]),
                                            windows(lo, D), ALU.mult)
                    if c == 1:
                        ins.then_inc(keys_multiplied, 1)
                    else:
                        st.did(ins)

                def add_channels(c):
                    st.settle()
                    st.did(dve.tensor_reduce(score[:, c * JC:(c + 1) * JC].rearrange("p j w h -> p (j w h)"),
                                             prod[:, keys_half[c]].rearrange("p j w (h d) -> p (j w h) d", d=DK), X, ALU.add))

                def subtract_max(h):
                    mine = score[:, h * HJ:(h + 1) * HJ]
                    st.settle()
                    if h == 0:
                        n = JC * W
                        first = mine[:, 0:JC].rearrange("p j w h -> p (j w) h")
                        st.did(dve.tensor_tensor(first, first, window_mask[:, 0:n].rearrange("p (n o) -> p n o", o=1)
                                                 .to_broadcast([P, n, HEADS]), ALU.add))
                        dve.wait_ge(channels_added, g + 1)
                        for a in range(2):
                            second = mine[:, JC + a * JC // 2:JC + (a + 1) * JC // 2]
                            mask = window_mask[:, n + a * n // 2:n + (a + 1) * n // 2]
                            st.did(dve.tensor_tensor(second.rearrange("p j w h -> p (j w) h"),
                                                     score_banks[:, a, :].rearrange("p (n h) -> p n h", h=HEADS),
                                                     mask.rearrange("p (n o) -> p n o", o=1)
                                                     .to_broadcast([P, n // 2, HEADS]), ALU.add))
                        st.settle()
                    st.did(dve.tensor_reduce(smax[:], mine.rearrange("p j w h -> p j h w"), X, ALU.max))
                    st.settle()
                    dve.tensor_tensor(mine, mine, smax[:].rearrange("p j (o h) -> p j o h", o=1)
                                      .to_broadcast([P, HJ, W, HEADS]), ALU.subtract).then_inc(score_ready, 1)

                def prob_value(c):
                    lo = c * JC
                    dve.wait_ge(prob_ready, g * 2 + (c // 2 + 1))
                    st.settle()
                    if c % 2:
                        dve.wait_ge(pv_summed, g * C + {1: 1, 3: 2}[c])
                    dve.tensor_tensor(prod[:, VALUES_HALF[c]].rearrange("p j w (h d) -> p j w h d", d=DK),
                                      score[:, lo:lo + JC].rearrange("p j w (h o) -> p j w h o", o=1)
                                      .to_broadcast([P, JC, W, HEADS, DK]),
                                      windows(lo, 2 * D, heads=True), ALU.mult).then_inc(pv_ready, 1)

                def add_probs(h):
                    n = HJ * HEADS
                    st.did(dve.tensor_reduce(ssum[:, h * n:(h + 1) * n].rearrange("p (j h) -> p j h", h=HEADS),
                                             score[:, h * HJ:(h + 1) * HJ].rearrange("p j w h -> p j h w"), X, ALU.add))
                    st.settle()
                    st.did(dve.reciprocal(sinv[:, h * n:(h + 1) * n], ssum[:, h * n:(h + 1) * n]))
                    st.settle()

                def take_o(c):
                    dve.wait_ge(pv_summed, g * C + (c + 1))
                    n = JC * HEADS
                    dve.tensor_tensor(o_sb[:, c * JC:(c + 1) * JC, :].rearrange("p j (h d) -> p (j h) d", d=DK),
                                      bank[6 + c % 2].rearrange("p (n d) -> p n d", d=DK),
                                      sinv[:, c * n:(c + 1) * n].rearrange("p (n o) -> p n o", o=1)
                                      .to_broadcast([P, n, DK]), ALU.mult).then_inc(o_ready, 1)

                def add_attention(c):
                    dve.wait_ge(attn_done, g * C + (c + 1))
                    here = xt(g * J + c * JC, JC)
                    dve.tensor_tensor(here, bank[4 + c % 2][:], here, ALU.add).then_inc(attn_added, 1)

                multiply_keys(0)
                add_channels(0)
                multiply_keys(1)
                multiply_keys(2)
                add_channels(2)
                subtract_max(0)
                prob_value(0)
                multiply_keys(3)
                add_channels(3)
                prob_value(1)
                subtract_max(1)
                add_probs(0)
                take_o(0)
                prob_value(2)
                take_o(1)
                prob_value(3)
                add_probs(1)
                if not last:
                    combine(g + 1, (g + 1) * J, (g + 1) * (J * 2), st, range(0, 2))
                take_o(2)
                if not last:
                    combine(g + 1, (g + 1) * J, (g + 1) * (J * 2), st, range(2, C))
                take_o(3)
                if last:
                    plan_tiles(1, 0, plan_in_y_in)
                    add_maps(SUMS, maps_in_y_in)
                if not last:
                    next_gather((g + 2) * (J * 2))
                add_attention(0)
                for c in range(1, C + 1):
                    if c < C:
                        add_attention(c)
                    dve.wait_ge(attn_added, g * C + c)
                    chunk_statistics(g * J, c - 1, st)

            def windows(lo, at, heads=False):
                a = qkv[:, lo:lo + 1, at:at + D]
                inner = [[DK, HEADS], [1, DK]] if heads else [[1, D]]
                return bass.AP(a.tensor, a.offset, [list(a.ap[0]), [3 * D, JC], [3 * D, W]] + inner)

            def split_weights(part):
                n = BLOCKS // 2
                dve.wait_ge(w_rounded, 2)
                dve.scalar_tensor_tensor(out=w_hl[:, bass.ds(part * n, n), 1, :], in0=w_stage[:, bass.ds(part * n, n), :],
                                         scalar=WS, in1=w_hl[:, bass.ds(part * n, n), 0, :],
                                         op0=ALU.mult, op1=ALU.subtract).then_inc(w_split, 1)

            plan_steps = Steps(dve, plan_step, 0)

            def planned(ins):
                plan_steps.did(ins)
                plan_steps.settle()

            def plan_tiles(f, h, m):
                did, e1 = planned, E + 1
                start = region
                if h == 1:
                    did(dve.tensor_copy(half_start[:], region[:]))
                    did(dve.tensor_copy(half_start[:, 0:E], group_end[:, (HG - 1) * E:HG * E]))
                    start = half_start
                end = group_end[:, ((h + 1) * HG - 1) * E:(h + 1) * HG * E]
                did(dve.tensor_tensor(plan_t[:, 0:E], end, start[:, 0:E], ALU.subtract))
                did(dve.tensor_scalar(counts_i[:], plan_t[:, 0:E], float(SLOT_TILE - 1), None, ALU.add))
                did(dve.tensor_scalar(n_tiles_i[:], counts_i[:], SLOT_TILE.bit_length() - 1, None, ALU.logical_shift_right))
                did(dve.tensor_copy(n_tiles[:], n_tiles_i[:]))
                did(dve.tensor_tensor(plan_t[:].rearrange("o (e f) -> o e f", f=E),
                                      earlier[:].rearrange("o (e f) -> o e f", f=E),
                                      n_tiles[:].rearrange("o (e f) -> o e f", e=1).to_broadcast([P, e1, E]), ALU.mult))
                did(dve.tensor_reduce(tile_start[:], plan_t[:].rearrange("o (e f) -> o e f", f=E), X, ALU.add))
                did(dve.scalar_tensor_tensor(out=row_off[:, h, :], in0=tile_start[:], scalar=-float(SLOT_TILE),
                                             in1=start[:], op0=ALU.mult, op1=ALU.add))
                tiles_bc = tile_no[:].rearrange("o (e n) -> o e n", e=1).to_broadcast([1, e1, HT])
                did(dve.memset(m.begun[:, e1 * HT:], 0.0))
                did(dve.tensor_tensor(m.begun[:, 0:e1 * HT].rearrange("o (e n) -> o e n", n=HT), tiles_bc,
                                      tile_start[0:1, :].rearrange("o (e n) -> o e n", n=1).to_broadcast([1, e1, HT]), ALU.is_ge))
                did(dve.tensor_tensor(m.mine, m.begun[:, 0:e1 * HT], m.begun[:, HT:], ALU.subtract))
                did(dve.tensor_tensor(m.mine_w.rearrange("o (e n) -> o e n", n=HT), m.mine.rearrange("o (e n) -> o e n", n=HT),
                                      row_off[0:1, h, :].rearrange("o (e n) -> o e n", n=1)
                                      .to_broadcast([1, e1, HT]), ALU.mult))
                did(dve.tensor_reduce(m.map_f[:, 0, :], m.mine_w.rearrange("o (e n) -> o n e", n=HT), X, ALU.add))
                did(dve.scalar_tensor_tensor(out=tile_row[:, h * HT:(h + 1) * HT], in0=tile_no[:], scalar=float(SLOT_TILE),
                                             in1=m.map_f[:, 0, :], op0=ALU.mult, op1=ALU.add))
                did(dve.tensor_reduce(m.map_f[:, 1, :], m.begun[:, HT:E * HT].rearrange("o (e n) -> o n e", n=HT), X, ALU.add))
                dve.tensor_copy(tile_expert[:, h * HT:(h + 1) * HT], m.map_f[:, 1, :]).then_inc(plan_ready, 1)
                if f == 0 and h == 1:
                    did(dve.tensor_copy(slot_base[:, 0, :], slot_base[:, 1, :]))

            def plan_rows(h):
                did, cols = planned, slice(h * PAIRS, (h + 1) * PAIRS)
                did(dve.tensor_tensor(row_jump[:, h, :], row_off[:, h, 1:], row_off[:, h, 0:E], ALU.subtract))
                did(dve.tensor_tensor(jumps[0], slots_all[:, cols].rearrange("p (n o) -> p n o", o=1).to_broadcast([P, PAIRS, E - 1]),
                                      region[:, 1:E].rearrange("p (o e) -> p o e", o=1).to_broadcast([P, PAIRS, E - 1]), ALU.is_ge))
                did(dve.tensor_tensor(jumps[1], jumps[0], row_jump[:, h, 0:E - 1].rearrange("p (o e) -> p o e", o=1)
                                      .to_broadcast([P, PAIRS, E - 1]), ALU.mult))
                did(dve.tensor_reduce(y_row_f, jumps[1], X, ALU.add))
                did(dve.scalar_tensor_tensor(out=y_row[:, cols], in0=slots_all[:, cols], scalar=row_off[:, h, 0:1], in1=y_row_f,
                                             op0=ALU.subtract, op1=ALU.subtract))

            def add_maps(u, maps):
                dve.wait_ge(maps_loaded, (u + 1) * NJ * DMA)
                carry_waits(dve)
                for r in range(1, NJ):
                    ins = dve.tensor_tensor(maps.sum, maps.four[:, 0, :] if r == 1 else maps.sum, maps.four[:, r, :],
                                            ALU.bitwise_or)
                    if r < NJ - 1:
                        ins.then_inc(maps_partly, 1)
                        dve.wait_ge(maps_partly, u * (NJ - 2) + r)
                ins.then_inc(maps_added, 1)

            def experts(f):
                last = Tile(0, NT - 1, f, NT)

                def copy_xT(t):
                    dve.wait_ge(xs_turned[t.ring], t.ring_uses + 1)
                    if t.par_reused:
                        dve.wait_ge(h_done[t.par], t.par_uses * 2)
                    dve.tensor_copy(xsT[:, t.par].rearrange("p s i n -> p (s i n)"),
                                    bank[t.par][:].bitcast(F16)[:, 0:4 * P]).then_inc(xsT_ready[t.par], 1)

                def split_h(t, b):
                    dve.wait_ge(h_hi[t.par], t.par_uses * 2 + (b + 1))
                    dve.tensor_tensor(h_hl[:, t.par, 1, 2 * b:2 * b + 2, :], h_f[:, t.par, 2 * b:2 * b + 2, :],
                                      h_hl[:, t.par, 0, 2 * b:2 * b + 2, :], ALU.subtract).then_inc(h_split[t.par], 1)

                def take_y(t, e):
                    dve.wait_ge(y_done, t.count + 1)
                    if t.ring_reused:
                        dve.wait_ge(y_stored[t.ring], t.ring_uses * DMA)
                    dve.scalar_tensor_tensor(
                        out=y_sb[:, t.ring], in0=y_banks[:, :, 0:D],
                        scalar=1.0 / WS, in1=b2_bc[:, bass.ds(e * D, D)].rearrange("p (o d) -> p o d", o=1)
                        .to_broadcast([P, 2, D]), op0=ALU.mult, op1=ALU.add).then_inc(y_begun, 1)
                    dve.wait_ge(y_begun, t.count + 1)
                    dve.scalar_tensor_tensor(out=y_sb[:, t.ring], in0=y_banks[:, :, D:2 * D], scalar=1.0 / WS,
                                             in1=y_sb[:, t.ring], op0=ALU.mult, op1=ALU.add).then_inc(y_ready, 1)

                def step(t, nxt, prv, old):
                    if not prv:
                        copy_xT(t)
                    if prv:
                        e = dve.value_load(tile_expert[0:1, bass.ds(prv.j, 1)], min_val=0, max_val=E - 1)
                    if nxt:
                        copy_xT(nxt)
                    split_h(t, 0)
                    if prv:
                        take_y(prv, e)
                    split_h(t, 1)

                def offer_along(i, k):
                    if k == -1:
                        offer_slots(False, i * (J // NJ) + (G * f + G - 1) * SC, i * J + (G - 1) * (2 * J), J)
                    elif k == SUM_TILE + 1:
                        add_maps(i + (SUMS * f + 1), maps_in_qkv)

                def combine_along(i, k):
                    nonlocal st
                    if k == -1:
                        st = Steps(dve, out_step, i * (2 * J // 2) + out_steps_before)
                    elif k in COMBINE_TILES:
                        combine(i + G, i * J, i * (J * 2), st, [COMBINE_TILES.index(k)])
                        if k == COMBINE_TILES[-1]:
                            next_gather(i * (J * 2) + J * 2)
                st = None
                before = {HT: lambda: plan_rows(0), HT + 2: lambda: plan_rows(1)}
                if f == 1:
                    before[HT + 5] = lambda: next_gather(0)
                dve.wait_ge(plan_ready, 2 * f + 2)
                over_expert_tiles(dve, f, step, before, offer_along, combine_along if f == 1 else None)
                take_y(last, dve.value_load(tile_expert[0:1, bass.ds(last.j, 1)], min_val=0, max_val=E - 1))

            def first_pass(g, weights=None):
                st = Steps(dve, route_step, g * ROUTE_STEPS)
                dve.wait_ge(x_loaded, (g + 1) * DMA)
                statistics(g * J, 0, st)
                if g > 1:
                    offer_slots(False, (g - 1) * SC, (g - 1) * (2 * J), 2 * J)
                norm(g, g * J, 0, st)
                if weights is not None:
                    split_weights(weights)
                low_halves(g)
                route(g, g, st)
                assert st.n == ROUTE_STEPS, st.n

            first_pass(0)
            offer_slots(True, 0, 0, 2 * J)
            first_pass(1)
            first_pass(HG, 0)
            plan_tiles(0, 0, plan_in_qkv)
            first_pass(HG + 1, 1)
            plan_tiles(0, 1, plan_in_qkv)
            add_maps(0, maps_in_qkv)
            experts(0)
            next_gather(0)
            st = Steps(dve, out_step, 0)
            combine(0, 0, 0, st)
            next_gather(J * 2)
            dve.wait_ge(combined, C)
            statistics(0, 1, st)
            norm(G, 0, 1, st)
            out_steps_before = st.n

            def second_pass(g, last):
                st = Steps(dve, group_step, g * GROUP_STEPS)
                attention(g, st, last)
                statistics(g * J, 0, st, chunks_done=True)
                norm(g * 2 + (G + 1), g * J, 0, st)
                if not last:
                    dve.wait_ge(combined, (g + 1) * C + C)
                    statistics((g + 1) * J, 1, st)
                low_halves(g + G)
                if not last:
                    dve.wait_ge(hl_ready, g + (G + 1))
                    dve.wait_ge(xn_turned, (g * 2 + (G + 2)) * C)
                    norm(g * 2 + (G + 2), (g + 1) * J, 1, st)
                route(g + G, g, st)
                if not last:
                    offer_slots(False, (g + G) * SC, g * (2 * J), 2 * J)
                assert last or st.n == GROUP_STEPS, st.n

            with dve.Fori(0, G - 1) as g:
                second_pass(g, False)
            second_pass(G - 1, True)
            plan_tiles(1, 1, plan_in_y_in)
            experts(1)
            with dve.Fori(HG, G) as g:
                st = Steps(dve, out_step, g * (2 * J // 2) + out_steps_before)
                combine(g + G, g * J, g * (J * 2), st)
                next_gather(g * (J * 2) + J * 2)


_INS = ["L0_attn_x", "L0_attn_Wq", "L0_attn_Wk", "L0_attn_Wv", "L0_attn_Wo", "L0_ffn_Wg", "L0_ffn_bg",
        "L0_ffn_W1", "L0_ffn_b1", "L0_ffn_W2", "L0_ffn_b2"]


def kernel(**inputs):
    import numpy as _np
    import concourse.bacc as _bacc
    from concourse import mybir as _mybir
    from concourse.bass_utils import run_bass_kernel_spmd as _run

    nc = _bacc.Bacc("TRN2", target_bir_lowering=False, num_devices=1)
    arrays, args = {}, []
    for name in _INS:
        a = _np.ascontiguousarray(inputs[name])
        arrays[f"in_{name}"] = a
        args.append(nc.dram_tensor(f"in_{name}", a.shape, _mybir.dt.from_np(a.dtype), kind="ExternalInput").ap())
    args.append(nc.dram_tensor("out_0", arrays["in_L0_attn_x"].shape, F32, kind="ExternalOutput").ap())
    macaron(nc, *args)
    r = _run(nc, [arrays], core_ids=[0])
    return r.results[0]["out_0"]
```
